# Optimizing a Trainium2 kernel written in Bass

```python
import numpy as np
import jax
import jax.numpy as jnp

def _softmax(x, axis=-1):
    return jax.nn.softmax(x, axis=axis)

def _gelu(x):
    return jax.nn.gelu(x, approximate=True)

def _silu(x):
    return jax.nn.silu(x)

def _sigmoid(x):
    return jax.nn.sigmoid(x)

def _layernorm(x, axis=-1, eps=1e-05):
    m = jnp.mean(x, axis=axis, keepdims=True)
    v = jnp.var(x, axis=axis, keepdims=True)
    return (x - m) / jnp.sqrt(v + eps)

def _scatter_add(tgt, idx, src, axis=0):
    return tgt.at[idx].add(src)

def _segment_sum(src, seg, n):
    return jax.ops.segment_sum(src, seg, n)
kernel_name = 'mk_early_fusion_d1_tok_img256_r4_0eaefa'

def setup_inputs(seed: int=0):
    np.random.seed(seed)
    _w = jnp.asarray

    def _rec_inputs():
        import jax
        import jax.numpy as jnp
        _rk = jax.random.key(seed)
        x = 7.57192e-06 + 1.00007 * jax.random.normal(jax.random.fold_in(_rk, 1), (16, 3, 224, 224), jnp.float32)
        txt = 0.00191194 + 0.0219993 * jax.random.normal(jax.random.fold_in(_rk, 2), (16, 32, 64), jnp.float32)
        return (x, txt)
    x, txt = _rec_inputs()

    def _L0_tok_setup():
        import jax, jax.numpy as jnp
        import numpy as np
        import math
        GRID = 28
        NUM_PATCHES = GRID * GRID
        PATCH = 8
        IN_CH = 3
        HIDDEN = 64
        BATCH = 64

        def build_grid_edges():
            edges = []
            for i in range(GRID):
                for j in range(GRID):
                    cur = i * GRID + j
                    if j < GRID - 1:
                        edges.append([cur, cur + 1])
                    if i < GRID - 1:
                        edges.append([cur, cur + GRID])
            e = np.asarray(edges, dtype=np.int32).T
            e = np.concatenate([e, e[::-1]], axis=1)
            return jnp.asarray(e)

        def sin_positional_encoding(n, d):
            pos = jnp.arange(n, dtype=jnp.float32)[:, None]
            div = jnp.exp(jnp.arange(0, d, 2, dtype=jnp.float32) * (-math.log(10000.0) / d))
            pe = jnp.zeros((n, d), dtype=jnp.float32)
            pe = pe.at[:, 0::2].set(jnp.sin(pos * div))
            pe = pe.at[:, 1::2].set(jnp.cos(pos * div))
            return pe
        key = jax.random.key(seed)
        ks = jax.random.split(key, 8)
        s = 0.02
        return {'x': jax.random.normal(ks[0], (BATCH, IN_CH, 224, 224), dtype=jnp.float32), 'W_embed': jax.random.normal(ks[1], (IN_CH * PATCH * PATCH, HIDDEN), dtype=jnp.float32) * s, 'b_embed': jax.random.normal(ks[2], (HIDDEN,), dtype=jnp.float32) * s, 'W_gcn': jax.random.normal(ks[3], (3, HIDDEN, HIDDEN), dtype=jnp.float32) * s, 'b_gcn': jax.random.normal(ks[4], (3, HIDDEN), dtype=jnp.float32) * s, 'W_out': jax.random.normal(ks[5], (HIDDEN, 64), dtype=jnp.float32) * s, 'b_out': jax.random.normal(ks[6], (64,), dtype=jnp.float32) * s, 'edge_index': build_grid_edges()}
    _L0_tok_all = _L0_tok_setup()
    _L0_tok_in = {k: v for k, v in _L0_tok_all.items() if k in ('W_embed', 'b_embed', 'W_gcn', 'b_gcn', 'W_out', 'b_out', 'edge_index')}
    del _L0_tok_all

    def _L0_attn_setup():
        import jax, jax.numpy as jnp
        import numpy as np
        HEADS = 8
        DIM = 64
        DIM_HEAD = 64
        DH = DIM_HEAD // HEADS
        SCALE = DIM_HEAD ** (-0.5)
        LN_EPS = 1e-05
        key = jax.random.key(seed)
        k1, k2, k3 = jax.random.split(key, 3)
        b, n = (8, 2048)
        x = jax.random.normal(k1, (b, n, DIM), dtype=jnp.float32)
        Wqkv = jax.random.normal(k2, (DIM, 3 * DIM_HEAD), dtype=jnp.float32) * 0.02
        Wout = jax.random.normal(k3, (DIM_HEAD, DIM), dtype=jnp.float32) * 0.02
        bout = jnp.zeros((DIM,), dtype=jnp.float32)
        gamma = jnp.ones((DIM,), dtype=jnp.float32)
        beta = jnp.zeros((DIM,), dtype=jnp.float32)
        return {'x': x, 'Wqkv': Wqkv, 'Wout': Wout, 'bout': bout, 'gamma': gamma, 'beta': beta}
    _L0_attn_all = _L0_attn_setup()
    _L0_attn_in = {k: v for k, v in _L0_attn_all.items() if k in ('Wqkv', 'Wout', 'bout', 'gamma', 'beta')}
    del _L0_attn_all

    def _L0_ffn_setup():
        import jax, jax.numpy as jnp
        import numpy as np
        B, S, H, F, E, K = (8, 1024, 64, 128, 16, 2)
        EPS = 1e-05
        key = jax.random.key(seed)
        ks = jax.random.split(key, 9)
        sc = 0.02
        return {'x': jax.random.normal(ks[0], (B, S, H), dtype=jnp.float32), 'gate_w': jax.random.normal(ks[1], (H, E), dtype=jnp.float32) * sc, 'gate_b': jnp.zeros((E,), dtype=jnp.float32), 'w1': jax.random.normal(ks[2], (E, H, F), dtype=jnp.float32) * sc, 'b1': jnp.zeros((E, F), dtype=jnp.float32), 'w2': jax.random.normal(ks[3], (E, F, H), dtype=jnp.float32) * sc, 'b2': jnp.zeros((E, H), dtype=jnp.float32), 'gamma': jnp.ones((H,), dtype=jnp.float32), 'beta': jnp.zeros((H,), dtype=jnp.float32)}
    _L0_ffn_all = _L0_ffn_setup()
    _L0_ffn_in = {k: v for k, v in _L0_ffn_all.items() if k in ('gate_w', 'gate_b', 'w1', 'b1', 'w2', 'b2', 'gamma', 'beta')}
    del _L0_ffn_all
    return {'x': x, 'txt': txt, 'L0_tok_W_embed': _L0_tok_in['W_embed'], 'L0_tok_b_embed': _L0_tok_in['b_embed'], 'L0_tok_W_gcn': _L0_tok_in['W_gcn'], 'L0_tok_b_gcn': _L0_tok_in['b_gcn'], 'L0_tok_W_out': _L0_tok_in['W_out'], 'L0_tok_b_out': _L0_tok_in['b_out'], 'L0_tok_edge_index': _L0_tok_in['edge_index'], 'L0_attn_Wqkv': _L0_attn_in['Wqkv'], 'L0_attn_Wout': _L0_attn_in['Wout'], 'L0_attn_bout': _L0_attn_in['bout'], 'L0_attn_gamma': _L0_attn_in['gamma'], 'L0_attn_beta': _L0_attn_in['beta'], 'L0_ffn_gate_w': _L0_ffn_in['gate_w'], 'L0_ffn_gate_b': _L0_ffn_in['gate_b'], 'L0_ffn_w1': _L0_ffn_in['w1'], 'L0_ffn_b1': _L0_ffn_in['b1'], 'L0_ffn_w2': _L0_ffn_in['w2'], 'L0_ffn_b2': _L0_ffn_in['b2'], 'L0_ffn_gamma': _L0_ffn_in['gamma'], 'L0_ffn_beta': _L0_ffn_in['beta']}

def reference(x, txt, L0_tok_W_embed, L0_tok_b_embed, L0_tok_W_gcn, L0_tok_b_gcn, L0_tok_W_out, L0_tok_b_out, L0_tok_edge_index, L0_attn_Wqkv, L0_attn_Wout, L0_attn_bout, L0_attn_gamma, L0_attn_beta, L0_ffn_gate_w, L0_ffn_gate_b, L0_ffn_w1, L0_ffn_b1, L0_ffn_w2, L0_ffn_b2, L0_ffn_gamma, L0_ffn_beta):
    import jax
    import jax.numpy as jnp

    def _L0_tok_ref(x, W_embed, b_embed, W_gcn, b_gcn, W_out, b_out, edge_index):
        import jax, jax.numpy as jnp
        import numpy as np
        import math
        GRID = 28
        NUM_PATCHES = GRID * GRID
        PATCH = 8
        IN_CH = 3
        HIDDEN = 64
        BATCH = 64

        def build_grid_edges():
            edges = []
            for i in range(GRID):
                for j in range(GRID):
                    cur = i * GRID + j
                    if j < GRID - 1:
                        edges.append([cur, cur + 1])
                    if i < GRID - 1:
                        edges.append([cur, cur + GRID])
            e = np.asarray(edges, dtype=np.int32).T
            e = np.concatenate([e, e[::-1]], axis=1)
            return jnp.asarray(e)

        def sin_positional_encoding(n, d):
            pos = jnp.arange(n, dtype=jnp.float32)[:, None]
            div = jnp.exp(jnp.arange(0, d, 2, dtype=jnp.float32) * (-math.log(10000.0) / d))
            pe = jnp.zeros((n, d), dtype=jnp.float32)
            pe = pe.at[:, 0::2].set(jnp.sin(pos * div))
            pe = pe.at[:, 1::2].set(jnp.cos(pos * div))
            return pe
        B = x.shape[0]
        N = NUM_PATCHES
        p = x.reshape(B, IN_CH, GRID, PATCH, GRID, PATCH)
        p = p.transpose(0, 2, 4, 1, 3, 5).reshape(B, N, IN_CH * PATCH * PATCH)
        h = p @ W_embed + b_embed + sin_positional_encoding(N, HIDDEN)[None]
        src, dst = (edge_index[0], edge_index[1])
        deg = jnp.zeros((N,), dtype=h.dtype).at[dst].add(1.0) + 1.0
        dinv = deg ** (-0.5)
        enorm = (dinv[src] * dinv[dst])[None, :, None]
        snorm = (1.0 / deg)[None, :, None]
        for i in range(3):
            hw = h @ W_gcn[i]
            agg = hw * snorm
            agg = agg.at[:, dst].add(hw[:, src] * enorm)
            h = jax.nn.relu(agg + b_gcn[i])
        return h @ W_out + b_out

    def _L0_attn_ref(x, Wqkv, Wout, bout, gamma, beta):
        import jax, jax.numpy as jnp
        import numpy as np
        HEADS = 8
        DIM = 64
        DIM_HEAD = 64
        DH = DIM_HEAD // HEADS
        SCALE = DIM_HEAD ** (-0.5)
        LN_EPS = 1e-05
        b, n, c = x.shape
        qkv = x @ Wqkv
        qkv = qkv.reshape(b, n, 3, HEADS, DH).transpose(2, 0, 3, 1, 4)
        q, k, v = (qkv[0], qkv[1], qkv[2])
        k = jax.nn.softmax(k, axis=-2)
        q = q * SCALE
        A = jnp.einsum('bhid,bhie->bhde', k, q)
        out = jnp.einsum('bhjd,bhde->bhje', v, A)
        out = out.reshape(b, n, c)
        out = out @ Wout + bout
        mu = jnp.mean(out, axis=-1, keepdims=True)
        var = jnp.var(out, axis=-1, keepdims=True)
        out = (out - mu) * jax.lax.rsqrt(var + LN_EPS) * gamma + beta
        return out

    def _L0_ffn_ref(x, gate_w, gate_b, w1, b1, w2, b2, gamma, beta):
        import jax, jax.numpy as jnp
        import numpy as np
        B, S, H, F, E, K = (8, 1024, 64, 128, 16, 2)
        EPS = 1e-05
        gate_logits = x @ gate_w + gate_b
        topk_vals, topk_idx = jax.lax.top_k(gate_logits, K)
        topk_w = jax.nn.softmax(topk_vals, axis=-1)
        h = jax.nn.relu(jnp.einsum('bsh,ehf->bsef', x, w1) + b1)
        expert_out = jnp.einsum('bsef,efh->bseh', h, w2) + b2
        sel = jnp.take_along_axis(expert_out, topk_idx[:, :, :, None], axis=2)
        moe = jnp.sum(topk_w[..., None] * sel, axis=2)
        y = x + moe
        mu = jnp.mean(y, axis=-1, keepdims=True)
        var = jnp.var(y, axis=-1, keepdims=True)
        return (y - mu) / jnp.sqrt(var + EPS) * gamma + beta
    h = _L0_tok_ref(x, L0_tok_W_embed, L0_tok_b_embed, L0_tok_W_gcn, L0_tok_b_gcn, L0_tok_W_out, L0_tok_b_out, L0_tok_edge_index)
    h = jnp.concatenate([h, txt], axis=1)
    h = h + _L0_attn_ref(_layernorm(h, axis=-1), L0_attn_Wqkv, L0_attn_Wout, L0_attn_bout, L0_attn_gamma, L0_attn_beta)
    h = h + _L0_ffn_ref(_layernorm(h, axis=-1), L0_ffn_gate_w, L0_ffn_gate_b, L0_ffn_w1, L0_ffn_b1, L0_ffn_w2, L0_ffn_b2, L0_ffn_gamma, L0_ffn_beta)
    return h

_drawn_inputs = setup_inputs


def setup_inputs(seed=0):
    import zlib

    import numpy as np

    out = dict(_drawn_inputs(seed))
    spreads = {'L0_attn_bout': (0.0, 0.1),
     'L0_attn_gamma': (1.0, 0.2),
     'L0_attn_beta': (0.0, 0.442),
     'L0_ffn_gate_b': (0.0, 0.1),
     'L0_ffn_b1': (0.0, 0.8),
     'L0_ffn_b2': (0.0, 0.8),
     'L0_ffn_gamma': (1.0, 0.546),
     'L0_ffn_beta': (0.0, 0.554)}
    factors = {'x': 8.0,
     'txt': 8.0,
     'L0_tok_W_embed': 8.0,
     'L0_tok_b_embed': 8.0,
     'L0_tok_W_gcn': 8.0,
     'L0_tok_b_gcn': 6.748,
     'L0_tok_W_out': 8.0,
     'L0_attn_Wqkv': 4.914,
     'L0_attn_Wout': 3.849,
     'L0_ffn_w1': 7.538,
     'L0_ffn_w2': 5.092,
     'L0_tok_b_out': 8.0}
    for name, (base, spread) in spreads.items():
        noise = np.random.default_rng([zlib.crc32(name.encode()), seed]).standard_normal(out[name].shape)
        drawn = base * np.exp(spread * noise) if base else spread * noise
        out[name] = jnp.asarray(drawn.astype(out[name].dtype))
    for name, factor in factors.items():
        out[name] = (out[name] * factor).astype(out[name].dtype)
    return out
```

```python
from contextlib import ExitStack
import math

import numpy as np

import concourse.bass as bass
from concourse import mybir
from concourse.alu_op_type import AluOpType as ALU

ACT = mybir.ActivationFunctionType
AX = mybir.AxisListType
F32 = mybir.dt.float32
F16 = mybir.dt.float16
BF16 = mybir.dt.bfloat16
I32 = mybir.dt.int32

GRID, PATCH, CH = 28, 8, 3
NODES = GRID * GRID
D = 64
TXT = 32
SEQ = NODES + TXT
IMAGES = 16
PAIRS = IMAGES // 2
HEADS, DH = 8, 8
TB = 112
NB = NODES // TB
TOK = SEQ // HEADS
NC = SEQ // TOK
LASTIMG = NODES - (NC - 1) * TOK
HALF = NODES // 2
RUN = PATCH // 2
KE = 2 * 2 * CH * PATCH
LAYERS = 3
EXPERTS, FF = 16, 128
GROUP = 4 * TOK
STEPS = 4 * EXPERTS
UNITS = STEPS // 2
EPS = 1e-5
SCALE = float(D) ** -0.5
TINY = 2.0 ** -60
HUGE = 3.0e38


def front_schedule():
    steps = []
    steps += [("embed", "pe", 0), ("embed", "pe", 1), ("embed_copy", "dve", 0)]
    for layer in range(LAYERS):
        steps.append(("node_mix", "pe", layer))
        steps.append(("node_copy", "dve", layer))
        steps.append(("aggregate", "pe", layer))
        steps.append(("graph_relu", "act", layer))
    steps += [("tokens", "pe", 0), ("tokens_copy", "dve", 0)]
    steps += [("ln_center", "dve", 0), ("ln_square", "act", 0), ("ln_var", "dve", 0), ("ln_rstd", "pool", 0),
              ("ln_apply", "dve", 0)]
    steps += [("x1_turn", "pe", 0), ("x1_copy", "act", 0), ("keys", "pe", 0), ("keys_max", "dve", 0),
              ("keys_exp", "act", 0), ("keys_turn", "pe", 0), ("keys_copy", "dve", 0), ("kx", "pe", 0),
              ("kx_copy", "dve", 0), ("kq", "pe", 0), ("kq_mask", "dve", 0), ("vkq", "pe", 0),
              ("vkq_copy", "dve", 0), ("heads", "pe", 0), ("heads_copy", "dve", 0), ("heads_copy", "act", 1),
              ("heads_turn", "pe", 0), ("heads_turned", "act", 0), ("attn_out", "pe", 0),
              ("attn_bias", "dve", 0)]
    steps += [("ln_center", "dve", 1), ("ln_square", "act", 1), ("ln_var", "dve", 1), ("ln_rstd", "pool", 1),
              ("ln_apply", "dve", 1), ("residual", "pool", 0)]
    steps += [("ln_center", "dve", 2), ("ln_square", "act", 2), ("ln_var", "dve", 2), ("ln_rstd", "pool", 2),
              ("ln_apply", "dve", 2)]
    steps += [("x2_split", "dve", 0), ("x2_turn", "pe", 0), ("x2_copy", "act", 0), ("logits", "pe", 0),
              ("top2_a", "dve", 0), ("top2_b", "dve", 0), ("top2_exp", "act", 0), ("top2_c", "dve", 0),
              ("gates_turn", "pe", 0), ("gates_copy", "dve", 0), ("bias2", "pe", 0), ("base", "dve", 0)]
    return steps


def build(nc, x, txt, W_embed, b_embed, W_gcn, b_gcn, W_out, b_out, edges, Wqkv, Wout, bout, ga, ba,
          gate_w, gate_b, w1, b1, w2, b2, gf, bf, c_ident, c_iota, c_node, c_mask, c_pos, out):
    E = edges.shape[1]
    EP = 126
    EC = E // EP
    assert EP * EC == E

    with ExitStack() as ctx:
        def sb(name, shape, dt=F32):
            return ctx.enter_context(nc.sbuf_tensor(name, shape, dt))

        def sem(name):
            return ctx.enter_context(nc.semaphore(name))

        F = ctx.enter_context(nc.psum_tensor("front", [128, 4, 512], F32))
        Z = ctx.enter_context(nc.psum_tensor("hidden_ps", [128, 2, 512], F32))
        O = ctx.enter_context(nc.psum_tensor("expert_ps", [128, 2, 512], F32))

        ident = sb("ident", [128, 128])
        ident16 = sb("ident16", [128, 128], F16)
        iota16 = sb("iota16", [128, NODES], F16)
        node = sb("node", [TB, NB])
        mask = sb("mask", [128, 128])
        pos = sb("pos", [128, NODES])
        wemb = sb("wemb", [KE, RUN, 2 * D])
        bemb = sb("bemb", [128, 1])
        wg = sb("wg", [128, LAYERS, 128])
        wtok = sb("wtok", [128, 128])
        wk = sb("wk", [128, 128])
        wq = sb("wq", [128, 128])
        wv = sb("wv", [128, 128])
        wvT = sb("wvT", [128, 128])
        watt = sb("watt", [128, 128])
        bg_rows = sb("bg_rows", [LAYERS, 2, D])
        bg = sb("bg", [128, LAYERS])
        btok = sb("btok", [TOK, D])
        batt = sb("batt", [TOK, D])
        ga_b = sb("ga_b", [TOK, D])
        ba_b = sb("ba_b", [TOK, D])
        gf_b = sb("gf_b", [TOK, D])
        bf_b = sb("bf_b", [TOK, D])
        gateb = sb("gateb", [TOK, EXPERTS])
        rev = sb("rev", [TOK, EXPERTS])
        mhalf = sb("mhalf", [128, NODES])
        gw = sb("gw", [128, EXPERTS])
        gwr = sb("gwr", [128, 2, EXPERTS])
        gw3 = sb("gw3", [128, 3, EXPERTS], BF16)
        w1max = sb("w1max", [FF, EXPERTS])
        w1pow = sb("w1pow", [FF, EXPERTS])
        w1inv = sb("w1inv", [FF, EXPERTS])
        w1s = sb("w1s", [128, 2, EXPERTS, FF], F16)
        b1n = sb("b1n", [EXPERTS, FF])
        b1s = sb("b1s", [FF, EXPERTS])
        w2s = sb("w2s", [FF, EXPERTS, D])
        b2d = sb("b2d", [128, NC, D])
        adj = sb("adj", [TB, NB, NODES])
        eidx = sb("eidx", [EP, 2, EC], I32)
        ef = sb("ef", [EP, 2, EC])
        shared = [[sb("shared_0", [128, EC * NODES]), 0], [sb("shared_1", [128, 10216]), 0]]

        alone = []

        def carve(area, shape, dt=F32):
            n = int(np.prod(shape[1:])) * (4 if dt == F32 else 2) // 4
            v = area[0][0:shape[0], area[1]:area[1] + n]
            area[1] += n
            if dt != F32:
                v = v.bitcast(dt)
            names = "abcde"[:len(shape) - 1]
            return v.rearrange(f"p ({' '.join(names)}) -> p {' '.join(names)}", **dict(zip(names, shape[1:])))

        def over(shape, dt=F32):
            n = int(np.prod(shape[1:])) * (4 if dt == F32 else 2) // 4
            for area in shared:
                if area[1] + n <= area[0].shape[1]:
                    return carve(area, shape, dt)
            alone.append(sb(f"alone_{len(alone)}", shape, dt))
            return alone[-1]

        hot = carve(shared[0], [EP, 2, EC, NODES], BF16)
        self_hot = carve(shared[1], [TB, NB, NODES], BF16)
        w1n = carve(shared[1], [D, EXPERTS, FF])
        w1sc = carve(shared[1], [FF, EXPERTS, D])
        w1T = carve(shared[1], [FF, 2, EXPERTS, 2, D], F16)
        deg = carve(shared[1], [TB, NODES])
        iota = carve(shared[1], [128, NODES])
        dinv = carve(shared[1], [TB, NODES])
        for area in shared:
            area[1] = 0
        ones = sb("ones", [128, 128], BF16)
        dsrc = sb("dsrc", [TB, NB])
        xt = sb("xt", [KE, GRID, GRID * PATCH])
        X = over([TB, NB, 2 * D])
        H = over([128, NODES])
        hL = sb("hL", [TOK, NC, 2, D])
        hb = over([TOK, NC, 2, D])
        xc = over([TOK, 2 * NC, D])
        sq = over([TOK, 2 * NC, D])
        st = sb("st", [TOK, LAYERS, 5, 2 * NC])
        x1 = over([TOK, NC, 2, D])
        x1T = over([128, NC, TOK])
        kneg = sb("kneg", [128, 1])
        ksum = sb("ksum", [128, 1])
        kinv = sb("kinv", [128, 1])
        ET = over([128, NC, TOK])
        Ek = over([TOK, NC, 128])
        kx = over([128, 128])
        kq = over([128, 128])
        vkq = over([128, 128])
        zh = Ek.rearrange("p c f -> p (c f)").rearrange("p (h t e) -> p h t e", h=2 * HEADS, t=NC)
        zT = ET
        yL = x1
        yn = over([TOK, NC, 2, D])
        x2s = over([TOK, NC, 2, 2, D], F16)
        lg = over([TOK, 2 * NC, EXPERTS])
        lg2 = over([TOK, 2 * NC, EXPERTS])
        hit = over([TOK, 2, 2 * NC, EXPERTS])
        ohot = over([TOK, 2, 2 * NC, EXPERTS])
        tv = sb("tv", [TOK, 10, 2 * NC])
        gT = over([128, 2, TOK])
        x2 = over([TOK, 2, NC, 2, D])
        hres = over([TOK, 2, NC, 2, D])
        x2T = sb("x2T", [128, 2, 2, SEQ], F16)
        gate = over([TOK, 2, 2 * NC, EXPERTS])
        base = over([TOK, 2, 2, NC, D])
        hid = over([FF, 4, GROUP])
        tmp = over([TOK, 2, 512])
        acc = over([TOK, 2, 4, 2, D])
        ys = over([TOK, NC, D])
        fxc = over([TOK, NC, D])
        fsq = over([TOK, NC, D])
        fst = sb("fst", [TOK, 5, NC])
        fin = over([TOK, 2, NC, D])

        s_const = sem("const_loaded")
        s_wz = sem("weights_zeroed")
        s_w = sem("weights_loaded")
        s_edge = sem("edges_loaded")
        s_wx = sem("expert_weights_loaded")
        s_ef = sem("edges_float")
        s_hot = sem("one_hots")
        s_oned = sem("ones_set")
        s_turn = sem("weights_turned")
        s_wcopy = sem("turned_copied")
        s_inv = sem("powers_inverted")
        s_posb = sem("pos_biased")
        s_w1t = sem("w1_turned")
        s_w1c = sem("w1_scaled")
        s_w1p = sem("w1_split_turned")
        s_w1s = sem("w1_ready")
        s_gw = sem("gate_weights_split")
        s_degs = sem("degree_sums")
        s_deg = sem("degrees")
        s_dinv = sem("degree_roots")
        s_dsrc = sem("source_roots")
        s_cnt = sem("edge_counts")
        s_adj = sem("adjacency")
        s_half = sem("exponent_set")
        counts = {
            "x_in": 192, "txt_in": 32, "embedded": 2, "embed": 2, "mixed": 6, "nodes": 6,
            "aggregated": 6, "graph": 6, "tokens_ps": 2, "tokens": 3, "stat": 9, "centred": 3, "squared": 3,
            "variance": 3, "rstd": 3, "normed": 3, "x1_turned": 2, "x1T_ready": 2, "keys_ps": 1, "kmax": 1,
            "kexp": 1, "keys_turned": 2, "keys_ready": 2, "kx_ps": 1, "kx_ready": 1, "kq_ps": 1, "kq_ready": 2,
            "vkq_ps": 1, "vkq_ready": 1, "heads_ps": 2, "heads_a": 1, "heads_b": 1, "heads_turned": 2,
            "zT_ready": 2, "attn_ps": 2, "attn": 2, "gam": 1, "hbeta": 1, "hres": 1, "x2_parts": 2, "x2_turned": 2, "x2T_ready": 2,
            "logits_ps": 2, "top2": 16, "top2b": 1, "top2_exp": 1, "gates": 4, "gates_turned": 1, "gates_ready": 1, "bias2_ps": 2,
            "base": 2,
            "hidden_ps": STEPS, "hidden": STEPS, "outputs_ps": UNITS, "gated": UNITS, "added": UNITS - 4,
            "folded": 4, "summed": 4, "f_stat": 6, "f_centred": 2, "f_squared": 2, "f_variance": 2, "f_rstd": 2,
            "f_normed": 2, "f_gamma": 2, "f_beta": 2, "final": 2, "stored": 32,
        }
        sems = {k: sem("s_" + k) for k in counts}

        def after(eng, name, p, k):
            v = p * counts[name] + k
            if isinstance(v, int) and v <= 0:
                return
            eng.wait_ge(sems[name], v)

        def bc(ap, n):
            return ap.unsqueeze(2).to_broadcast([ap.shape[0], ap.shape[1], n])

        def rows(ap, g):
            return ap.unsqueeze(1).to_broadcast([ap.shape[0], g, ap.shape[1]])

        def flat(ap):
            return ap.rearrange("p c b d -> p (c b) d")

        def bank16(i):
            return F[:, i, :].bitcast(F16)

        block = ctx.enter_context(nc.Block())

        @block.sync
        def _(sp):
            def row_bc(dst, src, n):
                return sp.dma_start(dst[0:TOK, :], src.partition_broadcast(TOK))

            sp.dma_start(eidx[:], edges.rearrange("a (p j) -> p a j", j=EC)).then_inc(s_edge, 16)
            for d, s in ((iota, c_iota), (node, c_node), (ident, c_ident), (mask, c_mask), (pos, c_pos)):
                sp.dma_start(d[:], s).then_inc(s_const, 16)

            def load_images(p):
                after(sp, "embedded", p, 0)
                for sh in range(2):
                    for b in range(2):
                        src = x[bass.ds(2 * p + b, 1)].rearrange("o c (i h) w -> (o c) h i w", h=PATCH)
                        w = GRID * PATCH - RUN * sh
                        for c in range(CH):
                            r = PATCH * (CH * (2 * sh + b) + c)
                            sp.dma_start(xt[r:r + PATCH, :, 0:w], src[c, :, :, RUN * sh:]
                                         ).then_inc(sems["x_in"], 16)

            load_images(0)
            sp.wait_ge(s_wz, 1)
            for b in range(2):
                r = slice(D * b, D * (b + 1))
                for sh in range(2):
                    q = CH * PATCH * (2 * sh + b)
                    sp.dma_start(wemb[q:q + CH * PATCH, :, r],
                                 W_embed.rearrange("(q w) d -> q w d", w=PATCH)[:, RUN * sh:RUN * (sh + 1), :]
                                 ).then_inc(s_w, 16)
                sp.dma_start(bemb[r, :], b_embed.rearrange("(d o) -> d o", o=1)).then_inc(s_w, 16)
                sp.dma_start(wg[r, :, r], W_gcn.rearrange("l k d -> k l d")).then_inc(s_w, 16)
                sp.dma_start(wtok[r, r], W_out).then_inc(s_w, 16)
                sp.dma_start(wq[r, r], Wqkv[:, 0:D]).then_inc(s_w, 16)
                sp.dma_start(wk[r, r], Wqkv[:, D:2 * D]).then_inc(s_w, 16)
                sp.dma_start(wv[r, r], Wqkv[:, 2 * D:3 * D]).then_inc(s_w, 16)
                sp.dma_start(watt[r, r], Wout).then_inc(s_w, 16)
                sp.dma_start(gw[r, :], gate_w).then_inc(s_w, 16)
                sp.dma_start(bg_rows[:, b, :], b_gcn).then_inc(s_w, 16)
            for d, s in ((btok, b_out), (batt, bout), (ga_b, ga), (ba_b, ba), (gf_b, gf), (bf_b, bf), (gateb, gate_b)):
                row_bc(d, s, s.shape[0]).then_inc(s_w, 16)
            sp.dma_start(w1n[:], w1.rearrange("e h f -> h e f")).then_inc(s_wx, 16)
            sp.dma_start(b1n[:], b1).then_inc(s_wx, 16)
            sp.dma_start(w2s[:], w2.rearrange("e f h -> f e h")).then_inc(s_wx, 16)
            for c in range(NC):
                sp.dma_start(b2d[EXPERTS * c:EXPERTS * (c + 1), c, :], b2).then_inc(s_wx, 16)

            def load_text(p):
                after(sp, "hbeta", p, 0)
                after(sp, "centred", p, 1 - 3)
                for b in range(2):
                    sp.dma_start(hL[LASTIMG:TOK, NC - 1, b, :], txt[bass.ds(2 * p + b, 1)].rearrange("o t d -> (o t) d")
                                 ).then_inc(sems["txt_in"], 16)

            def store(p, b):
                after(sp, "final", p, b + 1)
                sp.dma_start(out[bass.ds(2 * p + b, 1)].rearrange("o (c t) d -> (o t) c d", t=TOK), fin[:, b]
                             ).then_inc(sems["stored"], 16)

            load_text(0)
            load_images(1)
            with sp.Fori(1, PAIRS - 1) as p:
                load_text(p)
                load_images(p + 1)
                store(p - 1, 0)
                store(p - 1, 1)
            load_text(PAIRS - 1)
            for p in (PAIRS - 2, PAIRS - 1):
                store(p, 0)
                store(p, 1)
            sp.wait_ge(sems["stored"], 32 * PAIRS)

        def run(eng, name, front_step, ffn_step, ffn_end=None):
            steps = front_schedule()

            def body(front, par, ffn, fpar):
                for n in range(STEPS + 1):
                    if ffn is not None:
                        ffn_step(ffn, fpar, n)
                    if front is not None:
                        for k, (what, where, idx) in enumerate(steps):
                            if where == name and k * STEPS // len(steps) == n:
                                front_step(what, idx, front, par)

            body(0, 0, None, None)
            body(1, 1, 0, 0)
            with eng.Fori(0, (PAIRS - 2) // 2) as i:
                body(2 * i + 2, 0, 2 * i + 1, 1)
                body(2 * i + 3, 1, 2 * i + 2, 0)
            body(None, None, PAIRS - 1, 1)

        NW = 2 * 11 + 7

        @block.tensor
        def _(pe):
            mm, tr = pe.matmul, pe.transpose
            pe.wait_ge(s_const, 80)
            pe.wait_ge(s_w, 16 * NW)
            pe.wait_ge(s_wx, 16 * (3 + NC))
            tr(F[:, 0, 192:320], wv[:], ident[:])
            tr(F[:, 0, 320:336], b1n[:], ident[0:EXPERTS, 0:EXPERTS])
            tr(F[:, 0, 336:336 + LAYERS], bg_rows[:].rearrange("l b d -> l (b d)"), ident[0:LAYERS, 0:LAYERS]
               ).then_inc(s_turn, 1)
            for e in range(EXPERTS):
                t = tr(Z[:, e // 8, D * (e % 8):D * (e % 8 + 1)], w1n[:, e, :], ident[0:D, 0:D])
            t.then_inc(s_w1t, 1)
            pe.wait_ge(s_oned, 1)
            pe.wait_ge(s_hot, 2)
            pe.wait_ge(s_wcopy, 3)
            for h in range(2):
                for j in range(EC):
                    m = mm(F[0:TB, h, 0:HALF], ones[0:EP, 0:TB], hot[:, 1, j, HALF * h:HALF * (h + 1)],
                           start=(j == 0), stop=(j == EC - 1))
            m.then_inc(s_degs, 1)
            pe.wait_ge(s_hot, 3)
            for t in range(NB):
                for h in range(2):
                    q = 2 * t + h
                    bk = (q + 2) % 4
                    if q == 2:
                        pe.wait_ge(s_deg, 2)
                    if q >= 4:
                        pe.wait_ge(s_adj, q - 3)
                    for j in range(EC):
                        mm(F[0:TB, bk, 0:HALF], hot[:, 0, j, TB * t:TB * (t + 1)],
                           hot[:, 1, j, HALF * h:HALF * (h + 1)], start=(j == 0), stop=False)
                    mm(F[0:TB, bk, 0:HALF], self_hot[:, 0, 0:TB], self_hot[:, t, HALF * h:HALF * (h + 1)],
                       start=False, stop=True).then_inc(s_cnt, 1)
            pe.wait_ge(s_w1c, 6)
            for part in range(2):
                for e in range(EXPERTS):
                    dst = (O if part == 0 else Z)[:, e // 8, :].bitcast(F16)
                    t = tr(dst[:, FF * (e % 8):FF * (e % 8 + 1)], w1T[:, part, e].rearrange("f u k -> f (u k)"),
                           ident16[:])
                t.then_inc(s_w1p, 1)

            def front_step(what, idx, p, par):
                if what == "embed":
                    if idx == 0:
                        after(pe, "x_in", p, 192)
                        after(pe, "base", p, 0)
                        if isinstance(p, int) and p == 0:
                            pe.wait_ge(s_adj, 2 * NB)
                    v = xt[:].rearrange("p i (j w) -> p i j w", w=PATCH)
                    for w in range(RUN):
                        m = mm(F[:, 2 + idx, 0:HALF], wemb[:, w, :], v[:, 14 * idx:14 * idx + 14, :, w],
                               start=(w == 0), stop=(w == RUN - 1))
                    m.then_inc(sems["embedded"], 1)
                elif what == "node_mix":
                    if idx == 0:
                        after(pe, "embed", p, 2)
                    else:
                        after(pe, "graph", p, 2 * idx)
                    for t in range(NB):
                        m = mm(F[0:TB, t // 4, 128 * (t % 4):128 * (t % 4 + 1)], H[:, TB * t:TB * (t + 1)],
                               wg[:, idx, :], start=True, stop=True)
                        if t in (3, 6):
                            m.then_inc(sems["mixed"], 1)
                elif what == "aggregate":
                    after(pe, "nodes", p, 2 * idx + 2)
                    for h in range(2):
                        for t in range(NB):
                            m = mm(F[:, 2 + h, 0:HALF], X[:, t, :], adj[:, t, HALF * h:HALF * (h + 1)],
                                   start=(t == 0), stop=(t == NB - 1))
                        m.then_inc(sems["aggregated"], 1)
                elif what == "tokens":
                    after(pe, "graph", p, 6)
                    for c in range(NC):
                        n = TOK if c < NC - 1 else LASTIMG
                        m = mm(F[0:n, c // 4, 128 * (c % 4):128 * (c % 4 + 1)], H[:, TOK * c:TOK * c + n], wtok[:],
                               start=True, stop=True)
                        if c % 4 == 3:
                            m.then_inc(sems["tokens_ps"], 1)
                elif what == "x1_turn":
                    after(pe, "normed", p, 1)
                    for c in range(NC):
                        t = tr(F[:, 2 + c // 4, TOK * (c % 4):TOK * (c % 4 + 1)],
                               x1[:, c].rearrange("p b d -> p (b d)"), ident[0:TOK, 0:TOK])
                        if c % 4 == 3:
                            t.then_inc(sems["x1_turned"], 1)
                elif what == "keys":
                    after(pe, "x1T_ready", p, 2)
                    after(pe, "tokens", p, 3)
                    for h in range(2):
                        m = mm(F[:, h, 0:GROUP], wk[:], x1T[:, 4 * h:4 * h + 4, :].rearrange("p c t -> p (c t)"),
                               start=True, stop=True)
                    m.then_inc(sems["keys_ps"], 1)
                elif what == "keys_turn":
                    after(pe, "kexp", p, 1)
                    for c in range(NC):
                        t = tr(F[0:TOK, 2 + c // 4, 128 * (c % 4):128 * (c % 4 + 1)], ET[:, c, :], ident[:])
                        if c % 4 == 3:
                            t.then_inc(sems["keys_turned"], 1)
                elif what == "kx":
                    after(pe, "keys_ready", p, 2)
                    for c in range(NC):
                        m = mm(F[:, 0, 0:128], x1[:, c].rearrange("p b d -> p (b d)"), Ek[:, c, :],
                               start=(c == 0), stop=(c == NC - 1))
                    m.then_inc(sems["kx_ps"], 1)
                elif what == "kq":
                    after(pe, "kx_ready", p, 1)
                    mm(F[:, 2, 0:128], kx[:], wq[:], start=True, stop=True).then_inc(sems["kq_ps"], 1)
                elif what == "vkq":
                    after(pe, "kq_ready", p, 2)
                    mm(F[:, 0, 0:128], wvT[:], kq[:], start=True, stop=True).then_inc(sems["vkq_ps"], 1)
                elif what == "heads":
                    after(pe, "vkq_ready", p, 1)
                    xs = x1T[:].rearrange("p c t -> p (c t)").rearrange("p (m t) -> p t m", t=NC)
                    for t in range(NC):
                        m = mm(F[0:TOK, 2 + t // 4, 128 * (t % 4):128 * (t % 4 + 1)], xs[:, t, :], vkq[:],
                               start=True, stop=True)
                        if t % 4 == 3:
                            m.then_inc(sems["heads_ps"], 1)
                elif what == "heads_turn":
                    after(pe, "heads_a", p, 1)
                    after(pe, "heads_b", p, 1)
                    for hp in range(HEADS):
                        t = tr(F[:, hp // 4, TOK * (hp % 4):TOK * (hp % 4 + 1)],
                               zh[:, 2 * hp:2 * hp + 2].rearrange("p h t e -> p (h t e)"), ident[0:TOK, 0:TOK])
                        if hp % 4 == 3:
                            t.then_inc(sems["heads_turned"], 1)
                elif what == "attn_out":
                    after(pe, "zT_ready", p, 2)
                    for hp in range(HEADS):
                        m = mm(F[0:TOK, 2 + hp // 4, 128 * (hp % 4):128 * (hp % 4 + 1)], zT[:, hp, :], watt[:],
                               start=True, stop=True)
                        if hp % 4 == 3:
                            m.then_inc(sems["attn_ps"], 1)
                elif what == "x2_turn":
                    after(pe, "x2_parts", p, 2)
                    for b in range(2):
                        for c in range(NC):
                            t = tr(bank16(b)[:, TOK * c:TOK * (c + 1)], x2s[:, c, b].rearrange("p u d -> p (u d)"),
                                   ident16[0:TOK, 0:TOK])
                        t.then_inc(sems["x2_turned"], 1)
                elif what == "logits":
                    after(pe, "x2T_ready", p, 2)
                    if isinstance(p, int) and p == 0:
                        pe.wait_ge(s_gw, 6)
                    after(pe, "attn", p, 2)
                    for b in range(2):
                        for c in range(NC):
                            m = mm(F[0:TOK, 2 + b, 48 * c:48 * (c + 1)], x2T[:, par, b, TOK * c:TOK * (c + 1)],
                                   gw3[:].rearrange("p u e -> p (u e)"), start=True, stop=True)
                        m.then_inc(sems["logits_ps"], 1)
                elif what == "gates_turn":
                    after(pe, "gates", p, 4)
                    for b in range(2):
                        t = tr(F[:, 0, TOK * b:TOK * (b + 1)],
                               gate[:, par, NC * b:NC * (b + 1), :].rearrange("p c e -> p (c e)"), ident[0:TOK, 0:TOK])
                    t.then_inc(sems["gates_turned"], 1)
                elif what == "bias2":
                    after(pe, "gates_ready", p, 1)
                    for b in range(2):
                        mm(F[0:TOK, 2 + b, :], gT[:, b, :], b2d[:].rearrange("p c d -> p (c d)"),
                           start=True, stop=True).then_inc(sems["bias2_ps"], 1)

            def hidden(p, par, n):
                g, e = divmod(n, EXPERTS)
                if n == 0:
                    after(pe, "x2T_ready", p, 2)
                    if isinstance(p, int) and p == 0:
                        pe.wait_ge(s_w1s, 2)
                after(pe, "hidden", p, n - 1)
                for part in range(2):
                    m = mm(Z[:, n % 2, 0:GROUP], w1s[:, part, e, :],
                           x2T[:, par, g // 2, GROUP * (g % 2):GROUP * (g % 2 + 1)],
                           start=(part == 0), stop=(part == 1))
                m.then_inc(sems["hidden_ps"], 1)

            def ffn_step(p, par, n):
                if n == 0:
                    hidden(p, par, 0)
                if n + 1 < STEPS:
                    hidden(p, par, n + 1)
                if n == STEPS:
                    return
                u = n // 2
                if n % 2 == 0:
                    after(pe, "gated", p, u - 1)
                after(pe, "hidden", p, n + 1)
                for c in range(4):
                    m = mm(O[0:TOK, u % 2, 128 * c + D * (n % 2):128 * c + D * (n % 2 + 1)],
                           hid[:, n % 4, TOK * c:TOK * (c + 1)], w2s[:, n % EXPERTS, :], start=True, stop=True)
                if n % 2:
                    m.then_inc(sems["outputs_ps"], 1)

            run(pe, "pe", front_step, ffn_step)

        @block.scalar
        def _(act):
            act.wait_ge(s_w1p, 1)
            act.copy(w1s[:, 0].rearrange("p (h e) f -> p h (e f)", h=2), O[:].bitcast(F16)).then_inc(s_w1s, 1)
            act.wait_ge(s_w1p, 2)
            act.copy(w1s[:, 1].rearrange("p (h e) f -> p h (e f)", h=2), Z[:].bitcast(F16)).then_inc(s_w1s, 1)
            act.wait_ge(s_wcopy, 3)

            def front_step(what, idx, p, par):
                if what == "graph_relu":
                    for h in range(2):
                        after(act, "aggregated", p, 2 * idx + h + 1)
                        act.activation(H[:, HALF * h:HALF * (h + 1)], F[:, 2 + h, 0:HALF], ACT.Relu,
                                       bias=bg[:, idx:idx + 1]).then_inc(sems["graph"], 1)
                elif what == "ln_square":
                    after(act, "centred", p, idx + 1)
                    act.activation(sq[:], xc[:], ACT.Square).then_inc(sems["squared"], 1)
                elif what == "x1_copy":
                    for h in range(2):
                        after(act, "x1_turned", p, h + 1)
                        act.copy(x1T[:, 4 * h:4 * h + 4, :].rearrange("p c t -> p (c t)"), F[:, 2 + h, 0:GROUP]
                                 ).then_inc(sems["x1T_ready"], 1)
                elif what == "keys_exp":
                    after(act, "kmax", p, 1)
                    act.activation(ET[:].rearrange("p (h c) t -> p h (c t)", h=2), F[:, 0:2, 0:GROUP], ACT.Exp,
                                   bias=kneg[:], accum_out=ksum[:]).then_inc(sems["kexp"], 1)
                elif what == "heads_copy":
                    after(act, "heads_ps", p, 2)
                    act.copy(zh[:, :, 4:8, :].rearrange("p h t e -> p t h e"),
                             F[0:TOK, 3, :].rearrange("p (t h e) -> p t h e", t=4, e=DH)).then_inc(sems["heads_b"], 1)
                elif what == "heads_turned":
                    for h in range(2):
                        after(act, "heads_turned", p, h + 1)
                        act.copy(zT[:, 4 * h:4 * h + 4, :].rearrange("p c t -> p (c t)"), F[:, h, 0:GROUP]
                                 ).then_inc(sems["zT_ready"], 1)
                elif what == "x2_copy":
                    for b in range(2):
                        after(act, "x2_turned", p, b + 1)
                        act.copy(x2T[:, par, b, :], bank16(b)[:, 0:SEQ]).then_inc(sems["x2T_ready"], 1)
                elif what == "top2_exp":
                    after(act, "top2", p, 10)
                    act.activation(tv[:, 5], tv[:, 4], ACT.Exp).then_inc(sems["top2_exp"], 1)

            def ffn_step(p, par, n):
                if n < STEPS:
                    after(act, "hidden_ps", p, n + 1)
                    after(act, "outputs_ps", p, n // 2 - 1)
                    act.activation(hid[:, n % 4, :], Z[:, n % 2, 0:GROUP], ACT.Relu,
                                   bias=b1s[:, n % EXPERTS:n % EXPERTS + 1]).then_inc(sems["hidden"], 1)
                for b in range(2):
                    if n == (32 * (b + 1) + 3 if b == 0 else STEPS):
                        after(act, "f_centred", p, b + 1)
                        act.activation(fsq[:], fxc[:], ACT.Square).then_inc(sems["f_squared"], 1)

            run(act, "act", front_step, ffn_step)

        @block.vector
        def _(dve):
            tt, ts, cp = dve.tensor_tensor, dve.tensor_scalar, dve.tensor_copy
            dve.wait_ge(s_edge, 16)
            cp(ef[:], eidx[:]).then_inc(s_ef, 1)
            dve.wait_ge(s_const, 80)
            cp(iota16[:], iota).then_inc(s_ef, 1)
            cp(ident16[:], ident[:]).then_inc(s_ef, 1)
            dve.wait_ge(s_ef, 3)
            for a in (1, 0):
                for j in range(EC):
                    m = ts(hot[:, a, j, :], iota16[0:EP, :], ef[:, a, j:j + 1], None, ALU.is_equal)
                m.then_inc(s_hot, 1)
            for t in range(NB):
                m = ts(self_hot[:, t, :], iota16[0:TB, :], node[:, t:t + 1], None, ALU.is_equal)
            m.then_inc(s_hot, 1)
            dve.wait_ge(s_turn, 1)
            cp(wvT[:], F[:, 0, 192:320]).then_inc(s_wcopy, 1)
            cp(bg[:], F[:, 0, 336:336 + LAYERS]).then_inc(s_wcopy, 1)
            ts(pos[:], pos[:], bemb[:], None, ALU.add).then_inc(s_posb, 1)
            dve.wait_ge(s_w1t, 1)
            for h in range(2):
                dve.tensor_reduce(w1max[:, 8 * h:8 * h + 8], Z[:, h, :].rearrange("p (e k) -> p e k", k=D), AX.X,
                                  ALU.max, apply_absolute_value=True).then_inc(s_w1c, 1)
            dve.wait_ge(s_w1c, 2)
            ts(w1max[:], w1max[:], TINY, None, ALU.max).then_inc(s_w1c, 1)
            dve.wait_ge(s_w1c, 3)
            ts(w1pow[:].bitcast(I32), w1max[:].bitcast(I32), 0x7F800000, None, ALU.bitwise_and).then_inc(s_w1c, 1)
            dve.wait_ge(s_w1c, 4)
            dve.reciprocal(w1inv[:], w1pow[:]).then_inc(s_inv, 1)
            dve.wait_ge(s_inv, 1)
            tt(b1s[:], F[:, 0, 320:336], w1inv[:], ALU.mult).then_inc(s_wcopy, 1)
            for h in range(2):
                m = tt(w1sc[:, 8 * h:8 * h + 8, :], Z[:, h, :].rearrange("p (e k) -> p e k", k=D),
                       bc(w1inv[:, 8 * h:8 * h + 8], D), ALU.mult)
            m.then_inc(s_w1c, 1)
            tt(w2s[:], w2s[:], bc(w1pow[:], D), ALU.mult)
            dve.wait_ge(s_w1c, 5)
            for u in range(2):
                m = cp(w1T[:, 0, :, u, :], w1sc[:])
            m.then_inc(s_gw, 1)
            dve.wait_ge(s_gw, 1)
            for u in range(2):
                m = tt(w1T[:, 1, :, u, :], w1sc[:], w1T[:, 0, :, u, :], ALU.subtract)
            m.then_inc(s_w1c, 1)
            cp(gw3[:, 0, :], gw[:]).then_inc(s_gw, 1)
            dve.wait_ge(s_gw, 2)
            tt(gwr[:, 0, :], gw[:], gw3[:, 0, :], ALU.subtract).then_inc(s_gw, 1)
            dve.wait_ge(s_gw, 3)
            cp(gw3[:, 1, :], gwr[:, 0, :]).then_inc(s_gw, 1)
            dve.wait_ge(s_gw, 4)
            tt(gwr[:, 1, :], gwr[:, 0, :], gw3[:, 1, :], ALU.subtract).then_inc(s_gw, 1)
            dve.wait_ge(s_gw, 5)
            cp(gw3[:, 2, :], gwr[:, 1, :]).then_inc(s_gw, 1)
            dve.wait_ge(s_degs, 1)
            for h in range(2):
                ts(deg[:, HALF * h:HALF * (h + 1)], F[0:TB, h, 0:HALF], 1.0, None, ALU.add).then_inc(s_deg, 1)
            dve.wait_ge(s_dinv, 1)
            for t in range(NB):
                m = tt(adj[:, 0, TB * t:TB * (t + 1)], dinv[:, TB * t:TB * (t + 1)], ident[0:TB, 0:TB], ALU.mult)
            m.then_inc(s_dsrc, 1)
            dve.wait_ge(s_dsrc, 1)
            dve.tensor_reduce(dsrc[:], adj[:, 0, :].rearrange("p (t n) -> p t n", n=TB), AX.X, ALU.add
                              ).then_inc(s_dsrc, 1)
            dve.wait_ge(s_dsrc, 2)
            for t in range(NB):
                for h in range(2):
                    q = 2 * t + h
                    dve.wait_ge(s_cnt, q + 1)
                    dve.scalar_tensor_tensor(adj[:, t, HALF * h:HALF * (h + 1)], F[0:TB, (q + 2) % 4, 0:HALF],
                                             dsrc[:, t:t + 1], dinv[:, HALF * h:HALF * (h + 1)], ALU.mult, ALU.mult
                                             ).then_inc(s_adj, 1)

            def ln_center(src, dst_c, stats, groups, p, k, pre):
                base_n = 3 * k
                dve.tensor_reduce(stats[:, 0, 0:groups], src, AX.X, ALU.add).then_inc(sems[pre + "stat"], 1)
                after(dve, pre + "stat", p, base_n + 1)
                ts(stats[:, 1, 0:groups], stats[:, 0, 0:groups], -1.0 / D, None, ALU.mult
                   ).then_inc(sems[pre + "stat"], 1)
                after(dve, pre + "stat", p, base_n + 2)
                tt(dst_c, src, bc(stats[:, 1, 0:groups], D), ALU.add).then_inc(sems[pre + "centred"], 1)

            def ln_var(sqv, stats, groups, p, k, pre):
                after(dve, pre + "squared", p, k + 1)
                dve.tensor_reduce(stats[:, 2, 0:groups], sqv, AX.X, ALU.add).then_inc(sems[pre + "stat"], 1)
                after(dve, pre + "stat", p, 3 * k + 3)
                ts(stats[:, 3, 0:groups], stats[:, 2, 0:groups], 1.0 / D, EPS, ALU.mult, ALU.add
                   ).then_inc(sems[pre + "variance"], 1)

            def front_step(what, idx, p, par):
                if what == "embed_copy":
                    for h in range(2):
                        after(dve, "embedded", p, h + 1)
                        if h == 0:
                            after(dve, "tokens_ps", p, 0)
                            if isinstance(p, int) and p == 0:
                                dve.wait_ge(s_posb, 1)
                        n = slice(HALF * h, HALF * (h + 1))
                        tt(H[:, n], F[:, 2 + h, 0:HALF], pos[:, n], ALU.add).then_inc(sems["embed"], 1)
                elif what == "node_copy":
                    for h, (t0, t1) in enumerate(((0, 4), (4, 7))):
                        after(dve, "mixed", p, 2 * idx + h + 1)
                        if h == 0:
                            after(dve, "aggregated", p, 2 * idx)
                        cp(X[:, t0:t1, :].rearrange("p t f -> p (t f)"), F[0:TB, h, 0:128 * (t1 - t0)]
                           ).then_inc(sems["nodes"], 1)
                elif what == "tokens_copy":
                    after(dve, "tokens_ps", p, 2)
                    after(dve, "hbeta", p, 0)
                    after(dve, "txt_in", p, 32)
                    bt = rows(btok[:], 8)
                    tt(flat(hL[:, 0:4]), F[0:TOK, 0, :].rearrange("p (c d) -> p c d", d=D), bt, ALU.add
                       ).then_inc(sems["tokens"], 1)
                    tt(flat(hL[:, 4:7]), F[0:TOK, 1, 0:384].rearrange("p (c d) -> p c d", d=D), bt[:, 0:6], ALU.add
                       ).then_inc(sems["tokens"], 1)
                    tt(hL[0:LASTIMG, 7], F[0:LASTIMG, 1, 384:512].rearrange("p (c d) -> p c d", d=D),
                       bt[0:LASTIMG, 0:2], ALU.add).then_inc(sems["tokens"], 1)
                elif what == "ln_center":
                    if idx == 0:
                        after(dve, "tokens", p, 3)
                        src = flat(hL[:])
                    elif idx == 1:
                        after(dve, "attn", p, 2)
                        src = flat(yL[:])
                    else:
                        after(dve, "hres", p, 1)
                        src = flat(hres[:, par])
                    ln_center(src, xc[:], st[:, idx], 2 * NC, p, idx, "")
                elif what == "ln_var":
                    ln_var(sq[:], st[:, idx], 2 * NC, p, idx, "")
                elif what == "ln_apply":
                    after(dve, "rstd", p, idx + 1)
                    if idx == 2:
                        after(dve, "summed", p - 2, 4)
                    dst = (flat(x1[:]), flat(yn[:]), flat(x2[:, par]))[idx]
                    tt(dst, xc[:], bc(st[:, idx, 4], D), ALU.mult).then_inc(sems["normed"], 1)
                elif what == "keys_max":
                    after(dve, "keys_ps", p, 1)
                    dve.tensor_reduce(kneg[:], F[:, 0:2, 0:GROUP], AX.XY, ALU.max, negate=True
                                      ).then_inc(sems["kmax"], 1)
                elif what == "keys_copy":
                    for h in range(2):
                        after(dve, "keys_turned", p, h + 1)
                        cp(Ek[:, 4 * h:4 * h + 4, :].rearrange("p c f -> p (c f)"), F[0:TOK, 2 + h, :]
                           ).then_inc(sems["keys_ready"], 1)
                elif what == "kx_copy":
                    after(dve, "kx_ps", p, 1)
                    cp(kx[:], F[:, 0, 0:128]).then_inc(sems["kx_ready"], 1)
                elif what == "kq_mask":
                    dve.reciprocal(kinv[:], ksum[:]).then_inc(sems["kq_ready"], 1)
                    after(dve, "kq_ready", p, 1)
                    after(dve, "kq_ps", p, 1)
                    dve.scalar_tensor_tensor(kq[:], F[:, 2, 0:128], kinv[:], mask[:], ALU.mult, ALU.mult
                                             ).then_inc(sems["kq_ready"], 1)
                elif what == "vkq_copy":
                    after(dve, "vkq_ps", p, 1)
                    cp(vkq[:], F[:, 0, 0:128]).then_inc(sems["vkq_ready"], 1)
                elif what == "heads_copy":
                    after(dve, "heads_ps", p, 1)
                    cp(zh[:, :, 0:4, :].rearrange("p h t e -> p t h e"),
                       F[0:TOK, 2, :].rearrange("p (t h e) -> p t h e", t=4, e=DH)).then_inc(sems["heads_a"], 1)
                elif what == "attn_bias":
                    for b in range(2):
                        after(dve, "attn_ps", p, b + 1)
                        tt(yL[:, :, b, :], F[0:TOK, 2 + b, :].rearrange("p (c d) -> p c d", d=D), rows(batt[:], NC),
                           ALU.add).then_inc(sems["attn"], 1)
                elif what == "x2_split":
                    after(dve, "normed", p, 3)
                    v = x2[:, par]
                    cp(x2s[:, :, :, 0, :], v).then_inc(sems["x2_parts"], 1)
                    after(dve, "x2_parts", p, 1)
                    tt(x2s[:, :, :, 1, :], v, x2s[:, :, :, 0, :], ALU.subtract).then_inc(sems["x2_parts"], 1)
                elif what == "top2_a":
                    for b in range(2):
                        after(dve, "logits_ps", p, b + 1)
                        dve.tensor_reduce(lg[:, NC * b:NC * (b + 1), :],
                                          F[0:TOK, 2 + b, 0:48 * NC].rearrange("p (c u e) -> p c e u", u=3, e=EXPERTS),
                                          AX.X, ALU.add).then_inc(sems["top2"], 1)
                    after(dve, "top2", p, 2)
                    tt(lg[:], lg[:], rows(gateb[:], 2 * NC), ALU.add).then_inc(sems["top2"], 1)
                    after(dve, "top2", p, 3)
                    top(lg, 0, p, 3)
                elif what == "top2_b":
                    dve.scalar_tensor_tensor(lg2[:], ohot[:, 0], -HUGE, lg[:], ALU.mult, ALU.add
                                             ).then_inc(sems["top2"], 1)
                    after(dve, "top2", p, 8)
                    dve.tensor_reduce(tv[:, 1], lg2[:], AX.X, ALU.max).then_inc(sems["top2"], 1)
                    after(dve, "top2", p, 9)
                    tt(tv[:, 4], tv[:, 1], tv[:, 0], ALU.subtract).then_inc(sems["top2"], 1)
                    tt(hit[:, 1], lg2[:], bc(tv[:, 1], EXPERTS), ALU.is_equal).then_inc(sems["top2"], 1)
                    after(dve, "top2", p, 11)
                    tt(hit[:, 1], hit[:, 1], rows(rev[:], 2 * NC), ALU.mult).then_inc(sems["top2"], 1)
                    after(dve, "top2", p, 12)
                    dve.tensor_reduce(tv[:, 3], hit[:, 1], AX.X, ALU.max).then_inc(sems["top2"], 1)
                    after(dve, "top2", p, 13)
                    tt(ohot[:, 1], hit[:, 1], bc(tv[:, 3], EXPERTS), ALU.is_equal).then_inc(sems["top2"], 1)
                elif what == "top2_c":
                    after(dve, "top2_exp", p, 1)
                    ts(tv[:, 6], tv[:, 5], 1.0, None, ALU.add).then_inc(sems["top2"], 1)
                    after(dve, "top2", p, 15)
                    dve.reciprocal(tv[:, 7], tv[:, 6]).then_inc(sems["top2"], 1)
                    after(dve, "top2", p, 16)
                    tt(tv[:, 8], tv[:, 5], tv[:, 7], ALU.mult).then_inc(sems["gates"], 1)
                    tt(hit[:, 0], ohot[:, 0], bc(tv[:, 7], EXPERTS), ALU.mult).then_inc(sems["gates"], 1)
                    after(dve, "gates", p, 2)
                    tt(hit[:, 1], ohot[:, 1], bc(tv[:, 8], EXPERTS), ALU.mult).then_inc(sems["gates"], 1)
                    after(dve, "gates", p, 3)
                    tt(gate[:, par], hit[:, 0], hit[:, 1], ALU.add).then_inc(sems["gates"], 1)
                elif what == "gates_copy":
                    after(dve, "gates_turned", p, 1)
                    cp(gT[:].rearrange("p b t -> p (b t)"), F[:, 0, 0:2 * TOK]).then_inc(sems["gates_ready"], 1)
                elif what == "base":
                    for b in range(2):
                        after(dve, "bias2_ps", p, b + 1)
                        tt(base[:, par, b], x2[:, par, :, b, :], F[0:TOK, 2 + b, :].rearrange("p (c d) -> p c d", d=D),
                           ALU.add).then_inc(sems["base"], 1)

            def top(src, k, p, n0):
                dve.tensor_reduce(tv[:, k], src[:], AX.X, ALU.max).then_inc(sems["top2"], 1)
                after(dve, "top2", p, n0 + 1)
                tt(hit[:, k], src[:], bc(tv[:, k], EXPERTS), ALU.is_equal).then_inc(sems["top2"], 1)
                after(dve, "top2", p, n0 + 2)
                tt(hit[:, k], hit[:, k], rows(rev[:], 2 * NC), ALU.mult).then_inc(sems["top2"], 1)
                after(dve, "top2", p, n0 + 3)
                dve.tensor_reduce(tv[:, 2 + k], hit[:, k], AX.X, ALU.max).then_inc(sems["top2b"], 1)
                after(dve, "top2b", p, 1)
                tt(ohot[:, k], hit[:, k], bc(tv[:, 2 + k], EXPERTS), ALU.is_equal).then_inc(sems["top2"], 1)
                after(dve, "top2", p, n0 + 4)

            def ffn_step(p, par, n):
                if n < STEPS and n % 2 == 1:
                    u = n // 2
                    g, ep = divmod(u, 8)
                    after(dve, "outputs_ps", p, u + 1)
                    gv = gate[:, par, 4 * g:4 * g + 4, 2 * ep:2 * ep + 2]
                    gv = gv.unsqueeze(3).to_broadcast([TOK, 4, 2, D])
                    src = O[0:TOK, u % 2, :].rearrange("p (c e d) -> p c e d", c=4, e=2)
                    if ep == 0:
                        after(dve, "folded", p, g - 1)
                        dst = acc[:, g % 2]
                    else:
                        after(dve, "added", p, 7 * g + ep - 2 if ep >= 3 else 7 * g)
                        dst = tmp[:, ep % 2].rearrange("p (c e d) -> p c e d", c=4, e=2)
                    tt(dst, src, gv, ALU.mult).then_inc(sems["gated"], 1)
                for b in range(2):
                    at = 35 if b == 0 else STEPS
                    if n == at:
                        after(dve, "summed", p, 2 * b + 2)
                        ln_center(ys[:], fxc[:], fst, NC, p, b, "f_")
                        ln_var(fsq[:], fst, NC, p, b, "f_")
                        after(dve, "f_rstd", p, b + 1)
                        tt(fxc[:], fxc[:], bc(fst[:, 4, 0:NC], D), ALU.mult).then_inc(sems["f_normed"], 1)

            run(dve, "dve", front_step, ffn_step)

        @block.gpsimd
        def _(pool):
            tt = pool.tensor_tensor
            for w in (wemb, wg, wtok, wk, wq, wv, watt, b2d):
                m = pool.memset(w[:], 0.0)
            m.then_inc(s_wz, 1)
            pool.memset(ones[:], 1.0).then_inc(s_oned, 1)
            pool.memset(mhalf[:], -0.5).then_inc(s_half, 1)
            for e in range(EXPERTS):
                m = pool.memset(rev[:, e:e + 1], float(EXPERTS - e))
            m.then_inc(s_half, 1)
            pool.wait_ge(s_half, 2)
            pool.wait_ge(s_deg, 2)
            tt(dinv[:], deg[:], mhalf[0:TB, :], ALU.pow).then_inc(s_dinv, 1)
            pool.wait_ge(s_w, 16 * NW)

            def front_step(what, idx, p, par):
                if what == "ln_rstd":
                    after(pool, "variance", p, idx + 1)
                    tt(st[:, idx, 4], st[:, idx, 3], mhalf[0:TOK, 0:2 * NC], ALU.pow).then_inc(sems["rstd"], 1)
                    if idx == 0:
                        after(pool, "hres", p, 0)
                        tt(flat(hb[:]), flat(hL[:]), rows(ba_b[:], 2 * NC), ALU.add).then_inc(sems["hbeta"], 1)
                elif what == "residual":
                    after(pool, "normed", p, 2)
                    tt(flat(yn[:]), flat(yn[:]), rows(ga_b[:], 2 * NC), ALU.mult).then_inc(sems["gam"], 1)
                    after(pool, "gam", p, 1)
                    after(pool, "hbeta", p, 1)
                    after(pool, "final", p - 2, 2)
                    tt(flat(hres[:, par]), flat(yn[:]), flat(hb[:]), ALU.add).then_inc(sems["hres"], 1)

            def ffn_step(p, par, n):
                if n < STEPS and n % 2 == 1:
                    u = n // 2
                    g, ep = divmod(u, 8)
                    if ep:
                        a = acc[:, g % 2].rearrange("p c e d -> p (c e d)")
                        after(pool, "gated", p, u + 1)
                        after(pool, "added", p, 7 * g + ep - 1)
                        tt(a, a, tmp[:, ep % 2], ALU.add).then_inc(sems["added"], 1)
                    if ep == 7:
                        b, h = g // 2, g % 2
                        after(pool, "added", p, 7 * (g + 1))
                        if h == 0:
                            after(pool, "f_centred", p, b)
                        dst = ys[:, 4 * h:4 * h + 4, :]
                        tt(dst, acc[:, g % 2, :, 0, :], acc[:, g % 2, :, 1, :], ALU.add).then_inc(sems["folded"], 1)
                        after(pool, "folded", p, g + 1)
                        tt(dst, dst, base[:, par, b, 4 * h:4 * h + 4, :], ALU.add).then_inc(sems["summed"], 1)
                for b in range(2):
                    at = 36 if b == 0 else STEPS
                    if n == at:
                        after(pool, "f_variance", p, b + 1)
                        tt(fst[:, 4, 0:NC], fst[:, 3, 0:NC], mhalf[0:TOK, 0:NC], ALU.pow).then_inc(sems["f_rstd"], 1)
                        after(pool, "f_normed", p, b + 1)
                        tt(fxc[:], fxc[:], rows(gf_b[:], NC), ALU.mult).then_inc(sems["f_gamma"], 1)
                        after(pool, "f_gamma", p, b + 1)
                        tt(fxc[:], fxc[:], rows(bf_b[:], NC), ALU.add).then_inc(sems["f_beta"], 1)
                        after(pool, "f_beta", p, b + 1)
                        after(pool, "stored", p - 1, 32)
                        tt(fin[:, b], fxc[:], hres[:, par, :, b, :], ALU.add).then_inc(sems["final"], 1)

            run(pool, "pool", front_step, ffn_step)


def constants():
    pos = np.arange(NODES, dtype=np.float32)[:, None]
    div = np.exp(np.arange(0, D, 2, dtype=np.float32) * np.float32(-math.log(10000.0) / D))
    pe = np.zeros((NODES, D), np.float32)
    pe[:, 0::2] = np.sin(pos * div)
    pe[:, 1::2] = np.cos(pos * div)
    head = np.arange(128) // DH
    return {
        "ident": np.eye(128, dtype=np.float32),
        "iota": np.broadcast_to(np.arange(NODES, dtype=np.float32), (128, NODES)).copy(),
        "node": (np.arange(TB)[:, None] + TB * np.arange(NB)[None, :]).astype(np.float32),
        "mask": ((head[:, None] == head[None, :]) * SCALE).astype(np.float32),
        "pos": np.concatenate([pe.T, pe.T]),
    }


_INS = ["x", "txt", "L0_tok_W_embed", "L0_tok_b_embed", "L0_tok_W_gcn", "L0_tok_b_gcn", "L0_tok_W_out",
        "L0_tok_b_out", "L0_tok_edge_index", "L0_attn_Wqkv", "L0_attn_Wout", "L0_attn_bout", "L0_attn_gamma",
        "L0_attn_beta", "L0_ffn_gate_w", "L0_ffn_gate_b", "L0_ffn_w1", "L0_ffn_b1", "L0_ffn_w2", "L0_ffn_b2",
        "L0_ffn_gamma", "L0_ffn_beta"]


def kernel(**inputs):
    import concourse.bacc as _bacc
    from concourse.bass_utils import run_bass_kernel_spmd as _run

    nc = _bacc.Bacc("TRN2", target_bir_lowering=False, num_devices=1)
    arrays, args = {}, []
    for name in _INS:
        a = np.ascontiguousarray(inputs[name])
        arrays["in_" + name] = a
        args.append(nc.dram_tensor("in_" + name, a.shape, mybir.dt.from_np(a.dtype), kind="ExternalInput").ap())
    for name, a in constants().items():
        arrays["const_" + name] = a
        args.append(nc.dram_tensor("const_" + name, a.shape, mybir.dt.from_np(a.dtype), kind="ExternalInput").ap())
    out = nc.dram_tensor("out_0", (IMAGES, SEQ, D), F32, kind="ExternalOutput").ap()
    build(nc, *args, out)
    r = _run(nc, [arrays], core_ids=[0])
    return r.results[0]["out_0"]
```

```python
from contextlib import ExitStack
import math

import numpy as np

import concourse.bass as bass
from concourse import mybir
from concourse.alu_op_type import AluOpType as ALU

ACT = mybir.ActivationFunctionType
AX = mybir.AxisListType
F32 = mybir.dt.float32
F16 = mybir.dt.float16
BF16 = mybir.dt.bfloat16
I32 = mybir.dt.int32

GRID, PATCH, CH = 28, 8, 3
NODES = GRID * GRID
D = 64
TXT = 32
SEQ = NODES + TXT
IMAGES = 16
PAIRS = IMAGES // 2
HEADS, DH = 8, 8
TB = 112
NB = NODES // TB
TOK = SEQ // HEADS
NC = SEQ // TOK
LASTIMG = NODES - (NC - 1) * TOK
HALF = NODES // 2
RUN = PATCH // 2
KE = 2 * 2 * CH * PATCH
LAYERS = 3
EXPERTS, FF = 16, 128
GROUP = 4 * TOK
TMPS = 3
STEPS = 4 * EXPERTS
UNITS = STEPS // 2
REACH = GRID
EPS = 1e-5
SCALE = float(D) ** -0.5
TINY = 2.0 ** -60
HUGE = 3.0e38


def window(t):
    return max(0, TB * t - REACH), min(NODES, TB * (t + 1) + REACH)


LENGTH = {
    "embed": 28, "embed_copy": 12, "node_mix": 16, "node_copy": 12, "aggregate": 22, "graph_relu": 12, "tokens": 20,
    "tokens_copy": 14, "ln_center": 25, "ln_square": 12, "ln_var": 15, "ln_rstd": 28, "ln_apply": 13, "x1_turn": 10,
    "x1_copy": 13, "keys": 16, "keys_max": 11, "keys_exp": 12, "keys_turn": 12, "keys_copy": 13, "kx": 20,
    "kx_copy": 5, "kq": 5, "kq_mask": 6, "vkq": 5, "vkq_copy": 5, "heads": 20, "heads_copy": 6, "heads_turn": 10,
    "heads_turned": 13, "attn_out": 20, "attn_bias": 14, "residual": 26, "x2_split": 24, "x2_turn": 15,
    "x2_copy": 14, "logits": 15, "top2_a": 32, "top2_b": 32, "top2_exp": 5, "top2_c": 20, "gates_turn": 5,
    "gates_copy": 5, "bias2": 20, "base": 13,
}


HANDOVER = {("pe", "dve"): 8, ("pe", "act"): 8, ("dve", "pe"): 20, ("act", "pe"): 20, ("dve", "act"): 25,
            ("act", "dve"): 5, ("dve", "pool"): 5, ("pool", "dve"): 10}


def spread(steps, first, last):
    at, t = [], 0
    for k, (what, where, idx) in enumerate(steps):
        at.append(t)
        t += LENGTH[what]
        if k + 1 < len(steps):
            t += HANDOVER.get((where, steps[k + 1][1]), 0)
    return [(what, where, idx, first + a * (last - first) // at[-1]) for (what, where, idx), a in zip(steps, at)]


def graph_schedule():
    steps = [("embed", "pe", 0), ("embed", "pe", 1), ("embed_copy", "dve", 0)]
    for layer in range(LAYERS):
        steps += [("node_mix", "pe", layer), ("node_copy", "dve", layer), ("aggregate", "pe", layer),
                  ("graph_relu", "act", layer)]
    steps += [("tokens", "pe", 0), ("tokens_copy", "dve", 0)]
    return spread(steps, 0, STEPS - 2)


def attention_schedule():
    steps = [("ln_center", "dve", 0), ("ln_square", "act", 0), ("ln_var", "dve", 0), ("ln_rstd", "pool", 0),
             ("ln_apply", "dve", 0)]
    steps += [("x1_turn", "pe", 0), ("x1_copy", "act", 0), ("keys", "pe", 0), ("keys_max", "dve", 0),
              ("keys_exp", "act", 0), ("keys_turn", "pe", 0), ("keys_copy", "dve", 0), ("kx", "pe", 0),
              ("kx_copy", "dve", 0), ("kq", "pe", 0), ("kq_mask", "dve", 0), ("vkq", "pe", 0),
              ("vkq_copy", "dve", 0), ("heads", "pe", 0), ("heads_copy", "dve", 0), ("heads_copy", "act", 1),
              ("heads_turn", "pe", 0), ("heads_turned", "act", 0), ("attn_out", "pe", 0),
              ("attn_bias", "dve", 0)]
    steps += [("ln_center", "dve", 1), ("ln_square", "act", 1), ("ln_var", "dve", 1), ("ln_rstd", "pool", 1),
              ("ln_apply", "dve", 1), ("residual", "dve", 0)]
    steps += [("ln_center", "dve", 2), ("ln_square", "act", 2), ("ln_var", "dve", 2), ("ln_rstd", "pool", 2),
              ("ln_apply", "dve", 2)]
    steps += [("x2_split", "dve", 0), ("x2_turn", "pe", 0), ("x2_copy", "act", 0), ("logits", "pe", 0),
              ("top2_a", "dve", 0), ("top2_b", "dve", 0), ("top2_exp", "act", 0), ("top2_c", "dve", 0),
              ("gates_turn", "pe", 0), ("gates_copy", "dve", 0), ("bias2", "pe", 0), ("base", "dve", 0)]
    return spread(steps, 0, STEPS - 2)


def final_schedule():
    steps = []
    for b, first in ((0, STEPS // 2 + 1), (1, 1)):
        for what, where, lag in (("f_center", "dve", 0), ("f_square", "act", 3), ("f_var", "dve", 4),
                                 ("f_rstd", "pool", 5), ("f_apply", "dve", 8), ("f_gamma", "pool", 10),
                                 ("f_beta", "pool", 12), ("f_residual", "pool", 14)):
            steps.append((what, where, b, first + lag))
    return steps


def build(nc, x, txt, W_embed, b_embed, W_gcn, b_gcn, W_out, b_out, edges, Wqkv, Wout, bout, ga, ba,
          gate_w, gate_b, w1, b1, w2, b2, gf, bf, c_ident, c_iota, c_node, c_mask, c_pos, out):
    E = edges.shape[1]
    EP = 126
    EC = E // EP
    assert EP * EC == E

    with ExitStack() as ctx:
        def sb(name, shape, dt=F32):
            return ctx.enter_context(nc.sbuf_tensor(name, shape, dt))

        def sem(name):
            return ctx.enter_context(nc.semaphore(name))

        F = ctx.enter_context(nc.psum_tensor("front", [128, 4, 512], F32))
        Z = ctx.enter_context(nc.psum_tensor("hidden_ps", [128, 2, 512], F32))
        O = ctx.enter_context(nc.psum_tensor("expert_ps", [128, 2, 512], F32))

        ident = sb("ident", [128, 128])
        ident16 = sb("ident16", [128, 128], F16)
        iota16 = sb("iota16", [128, NODES], F16)
        node = sb("node", [TB, NB])
        mask = sb("mask", [128, 128])
        pos = sb("pos", [128, NODES])
        wemb = sb("wemb", [KE, RUN, 2 * D])
        bemb = sb("bemb", [128, 1])
        wg = sb("wg", [128, LAYERS, 128])
        wtok = sb("wtok", [128, 128])
        wk = sb("wk", [128, 128])
        wq = sb("wq", [128, 128])
        wv = sb("wv", [128, 128])
        wvT = sb("wvT", [128, 128])
        watt = sb("watt", [128, 128])
        bg_rows = sb("bg_rows", [LAYERS, 2, D])
        bg = sb("bg", [128, LAYERS])
        btok = sb("btok", [TOK, D])
        batt = sb("batt", [TOK, D])
        ga_b = sb("ga_b", [TOK, D])
        ba_b = sb("ba_b", [TOK, D])
        gf_b = sb("gf_b", [TOK, D])
        bf_b = sb("bf_b", [TOK, D])
        gateb = sb("gateb", [TOK, EXPERTS])
        rev = sb("rev", [TOK, EXPERTS])
        mhalf = sb("mhalf", [128, 2 * NC])
        gw = sb("gw", [128, EXPERTS])
        gwr = sb("gwr", [128, 2, EXPERTS])
        gw3 = sb("gw3", [128, 3, EXPERTS], BF16)
        w1max = sb("w1max", [FF, EXPERTS])
        w1pow = sb("w1pow", [FF, EXPERTS])
        w1inv = sb("w1inv", [FF, EXPERTS])
        w1s = sb("w1s", [128, 2, EXPERTS, FF], F16)
        b1n = sb("b1n", [EXPERTS, FF])
        b1s = sb("b1s", [FF, EXPERTS])
        w2s = sb("w2s", [FF, EXPERTS, D])
        b2d = sb("b2d", [128, NC, D])
        adj = sb("adj", [TB, NB, NODES])
        eidx = sb("eidx", [EP, 2, EC], I32)
        ef = sb("ef", [EP, 2, EC])
        shared = [[sb("shared_0", [128, EC * NODES]), 0], [sb("shared_1", [128, 10216]), 0]]

        alone = []

        def carve(area, shape, dt=F32):
            n = int(np.prod(shape[1:])) * (4 if dt == F32 else 2) // 4
            v = area[0][0:shape[0], area[1]:area[1] + n]
            area[1] += n
            if dt != F32:
                v = v.bitcast(dt)
            names = "abcde"[:len(shape) - 1]
            return v.rearrange(f"p ({' '.join(names)}) -> p {' '.join(names)}", **dict(zip(names, shape[1:])))

        def over(shape, dt=F32):
            n = int(np.prod(shape[1:])) * (4 if dt == F32 else 2) // 4
            for area in shared:
                if area[1] + n <= area[0].shape[1]:
                    return carve(area, shape, dt)
            alone.append(sb(f"alone_{len(alone)}", shape, dt))
            return alone[-1]

        hot = carve(shared[0], [EP, 2, EC, NODES], BF16)
        self_hot = carve(shared[1], [TB, NB, NODES], BF16)
        w1n = carve(shared[1], [D, EXPERTS, FF])
        w1sc = carve(shared[1], [FF, EXPERTS, D])
        w1T = carve(shared[1], [FF, 2, EXPERTS, 2, D], F16)
        ddiag = carve(shared[1], [TB, NB, TB])
        iota = carve(shared[1], [128, NODES])
        dinv = carve(shared[1], [TB, NODES])
        for area in shared:
            area[1] = 0
        one16 = sb("one16", [128, 1], BF16)
        ones = sb("ones", [TB, TB])
        reach = sb("reach", [EP, EC + 1])
        far_max = sb("far_max", [1, 1])
        far = sb("far", [1, 1], I32)
        degc = sb("degc", [TB, NB])
        dsrc = sb("dsrc", [TB, NB])
        xt = sb("xt", [KE, GRID, GRID * PATCH])
        X = over([TB, NB, 2 * D])
        H = over([128, NODES])
        hL = sb("hL", [TOK, NC, 2, D])
        hb = over([TOK, NC, 2, D])
        xc = over([TOK, 2 * NC, D])
        sq = over([TOK, 2 * NC, D])
        st = sb("st", [TOK, LAYERS, 5, 2 * NC])
        x1 = over([TOK, NC, 2, D])
        x1T = over([128, NC, TOK])
        kneg = sb("kneg", [128, 1])
        ksum = sb("ksum", [128, 1])
        kinv = sb("kinv", [128, 1])
        ET = over([128, NC, TOK])
        Ek = over([TOK, NC, 128])
        kx = over([128, 128])
        kq = over([128, 128])
        vkq = over([128, 128])
        zh = Ek.rearrange("p c f -> p (c f)").rearrange("p (h t e) -> p h t e", h=2 * HEADS, t=NC)
        zT = ET
        yL = x1
        yn = over([TOK, NC, 2, D])
        x2s = over([TOK, NC, 2, 2, D], F16)
        lg = over([TOK, 2 * NC, EXPERTS])
        lg2 = over([TOK, 2 * NC, EXPERTS])
        hit = over([TOK, 2, 2 * NC, EXPERTS])
        ohot = over([TOK, 2, 2 * NC, EXPERTS])
        tv = sb("tv", [TOK, 10, 2 * NC])
        gT = over([128, 2, TOK])
        x2 = over([TOK, 2, NC, 2, D])
        hres = over([TOK, 2, NC, 2, D])
        x2T = sb("x2T", [128, 2, 2, SEQ], F16)
        gate = over([TOK, 2, 2 * NC, EXPERTS])
        base = over([TOK, 2, 2, NC, D])
        hid = over([FF, 4, GROUP])
        tmp = over([TOK, TMPS, 512])
        acc = over([TOK, 2, 4, 2, D])
        ys = over([TOK, NC, D])
        fxc = over([TOK, NC, D])
        fst = sb("fst", [TOK, 5, NC])
        fin = over([TOK, 2, NC, D])

        s_const = sem("const_loaded")
        s_wz = sem("weights_zeroed")
        s_w = sem("weights_loaded")
        s_edge = sem("edges_loaded")
        s_wx = sem("expert_weights_loaded")
        s_ef = sem("edges_float")
        s_hot = sem("one_hots")
        s_oned = sem("ones_set")
        s_turn = sem("weights_turned")
        s_wcopy = sem("turned_copied")
        s_inv = sem("powers_inverted")
        s_posb = sem("pos_biased")
        s_w1t = sem("w1_turned")
        s_w1c = sem("w1_scaled")
        s_w1p = sem("w1_split_turned")
        s_w1s = sem("w1_ready")
        s_gw = sem("gate_weights_split")
        s_degs = sem("degree_sums")
        s_deg = sem("degrees")
        s_dsrc = sem("source_roots")
        s_ddiag = sem("roots_on_diagonals")
        s_dinv_ps = sem("roots_spread")
        s_dinv = sem("target_roots")
        s_reach = sem("edge_reach")
        s_reachT = sem("edge_reach_turned")
        s_far = sem("far_edges_known")
        s_cnt = sem("edge_counts")
        s_adj = sem("adjacency")
        s_half = sem("exponent_set")
        counts = {
            "x_in": 192, "txt_in": 32, "embedded": 2, "embed": 2, "mixed": 6, "nodes": 6,
            "aggregated": 6, "graph": 6, "tokens_ps": 2, "tokens": 3, "stat": 9, "centred": 3, "squared": 3,
            "variance": 3, "rstd": 3, "normed": 3, "x1_turned": 2, "x1T_ready": 2, "keys_ps": 1, "kmax": 1,
            "kexp": 1, "keys_turned": 2, "keys_ready": 2, "kx_ps": 1, "kx_ready": 1, "kq_ps": 1, "kq_ready": 2,
            "vkq_ps": 1, "vkq_ready": 1, "heads_ps": 2, "heads_a": 1, "heads_b": 1, "heads_turned": 2,
            "zT_ready": 2, "attn_ps": 2, "attn": 2, "gam": 1, "hbeta": 1, "hres": 1, "x2_parts": 2, "x2_turned": 2, "x2T_ready": 2,
            "logits_ps": 2, "top2": 16, "top2b": 1, "top2_exp": 1, "gates": 4, "gates_turned": 1, "gates_ready": 1, "bias2_ps": 2,
            "base": 2,
            "hidden_ps": STEPS, "hidden": STEPS, "outputs_ps": UNITS, "gated": UNITS, "added": UNITS - 4,
            "folded": 4, "summed": 4, "f_stat": 6, "f_centred": 2, "f_squared": 2, "f_variance": 2, "f_rstd": 2,
            "f_normed": 2, "f_gamma": 2, "f_beta": 2, "final": 2, "stored": 32,
        }
        sems = {k: sem("s_" + k) for k in counts}

        def after(eng, name, p, k):
            v = p * counts[name] + k
            if isinstance(v, int) and v <= 0:
                return
            eng.wait_ge(sems[name], v)

        def bc(ap, n):
            return ap.unsqueeze(2).to_broadcast([ap.shape[0], ap.shape[1], n])

        def rows(ap, g):
            return ap.unsqueeze(1).to_broadcast([ap.shape[0], g, ap.shape[1]])

        def flat(ap):
            return ap.rearrange("p c b d -> p (c b) d")

        def bank16(i):
            return F[:, i, :].bitcast(F16)

        block = ctx.enter_context(nc.Block())

        @block.sync
        def _(sp):
            def row_bc(dst, src, n):
                return sp.dma_start(dst[0:TOK, :], src.partition_broadcast(TOK))

            sp.dma_start(eidx[:], edges.rearrange("a (p j) -> p a j", j=EC)).then_inc(s_edge, 16)
            for d, s in ((iota, c_iota), (node, c_node), (ident, c_ident), (mask, c_mask), (pos, c_pos)):
                sp.dma_start(d[:], s).then_inc(s_const, 16)

            def load_images(p):
                after(sp, "embedded", p, 0)
                for sh in range(2):
                    for b in range(2):
                        src = x[bass.ds(2 * p + b, 1)].rearrange("o c (i h) w -> (o c) h i w", h=PATCH)
                        w = GRID * PATCH - RUN * sh
                        for c in range(CH):
                            r = PATCH * (CH * (2 * sh + b) + c)
                            sp.dma_start(xt[r:r + PATCH, :, 0:w], src[c, :, :, RUN * sh:]
                                         ).then_inc(sems["x_in"], 16)

            load_images(0)
            sp.wait_ge(s_wz, 1)
            for b in range(2):
                r = slice(D * b, D * (b + 1))
                for sh in range(2):
                    q = CH * PATCH * (2 * sh + b)
                    sp.dma_start(wemb[q:q + CH * PATCH, :, r],
                                 W_embed.rearrange("(q w) d -> q w d", w=PATCH)[:, RUN * sh:RUN * (sh + 1), :]
                                 ).then_inc(s_w, 16)
                sp.dma_start(bemb[r, :], b_embed.rearrange("(d o) -> d o", o=1)).then_inc(s_w, 16)
                sp.dma_start(wg[r, :, r], W_gcn.rearrange("l k d -> k l d")).then_inc(s_w, 16)
                sp.dma_start(wtok[r, r], W_out).then_inc(s_w, 16)
                sp.dma_start(wq[r, r], Wqkv[:, 0:D]).then_inc(s_w, 16)
                sp.dma_start(wk[r, r], Wqkv[:, D:2 * D]).then_inc(s_w, 16)
                sp.dma_start(wv[r, r], Wqkv[:, 2 * D:3 * D]).then_inc(s_w, 16)
                sp.dma_start(watt[r, r], Wout).then_inc(s_w, 16)
                sp.dma_start(gw[r, :], gate_w).then_inc(s_w, 16)
                sp.dma_start(bg_rows[:, b, :], b_gcn).then_inc(s_w, 16)
            for d, s in ((btok, b_out), (batt, bout), (ga_b, ga), (ba_b, ba), (gf_b, gf), (bf_b, bf), (gateb, gate_b)):
                row_bc(d, s, s.shape[0]).then_inc(s_w, 16)
            sp.dma_start(w1n[:], w1.rearrange("e h f -> h e f")).then_inc(s_wx, 16)
            sp.dma_start(b1n[:], b1).then_inc(s_wx, 16)
            sp.dma_start(w2s[:], w2.rearrange("e f h -> f e h")).then_inc(s_wx, 16)
            for c in range(NC):
                sp.dma_start(b2d[EXPERTS * c:EXPERTS * (c + 1), c, :], b2).then_inc(s_wx, 16)

            def load_text(p):
                after(sp, "hbeta", p, 0)
                after(sp, "centred", p, 1 - 3)
                for b in range(2):
                    sp.dma_start(hL[LASTIMG:TOK, NC - 1, b, :], txt[bass.ds(2 * p + b, 1)].rearrange("o t d -> (o t) d")
                                 ).then_inc(sems["txt_in"], 16)

            def store(p, b):
                after(sp, "final", p, b + 1)
                sp.dma_start(out[bass.ds(2 * p + b, 1)].rearrange("o (c t) d -> (o t) c d", t=TOK), fin[:, b]
                             ).then_inc(sems["stored"], 16)

            load_text(0)
            load_images(1)
            for p in (1, 2):
                load_text(p)
                load_images(p + 1)
            store(0, 0)
            with sp.Fori(3, PAIRS - 1) as p:
                load_text(p)
                load_images(p + 1)
                store(p - 3, 1)
                store(p - 2, 0)
            load_text(PAIRS - 1)
            for p in range(PAIRS - 4, PAIRS):
                if p > PAIRS - 4:
                    store(p, 0)
                store(p, 1)
            sp.wait_ge(sems["stored"], 32 * PAIRS)

        def run(eng, name, front_step, ffn_step, final_step):
            graph, attention, final = graph_schedule(), attention_schedule(), final_schedule()

            def body(ahead, front, par, ffn, fpar, tail):
                for n in range(STEPS):
                    if ffn is not None:
                        ffn_step(ffn, fpar, n)
                        for what, where, b, slot in final:
                            if where == name and slot == n and b == 0:
                                final_step(what, ffn, fpar, b)
                    if tail:
                        finish(ffn - 1, 1 - fpar, n)
                    for pair, steps in ((front, attention), (ahead, graph)):
                        if pair is not None:
                            for what, where, idx, slot in steps:
                                if where == name and slot == n:
                                    front_step(what, idx, pair, par)

            def finish(p, fpar, n):
                for what, where, b, slot in final:
                    if where == name and slot == n and b == 1:
                        final_step(what, p, fpar, b)

            body(0, None, None, None, None, False)
            body(1, 0, 0, None, None, False)
            body(2, 1, 1, 0, 0, False)
            with eng.Fori(0, (PAIRS - 4) // 2) as i:
                body(2 * i + 3, 2 * i + 2, 0, 2 * i + 1, 1, True)
                body(2 * i + 4, 2 * i + 3, 1, 2 * i + 2, 0, True)
            body(PAIRS - 1, PAIRS - 2, 0, PAIRS - 3, 1, True)
            body(None, PAIRS - 1, 1, PAIRS - 2, 0, True)
            body(None, None, None, PAIRS - 1, 1, True)
            for n in range(STEPS):
                finish(PAIRS - 1, 1, n)

        NW = 2 * 11 + 7

        @block.tensor
        def _(pe):
            mm, tr = pe.matmul, pe.transpose
            pe.wait_ge(s_const, 80)
            pe.wait_ge(s_w, 16 * NW)
            pe.wait_ge(s_wx, 16 * (3 + NC))
            tr(F[:, 0, 192:320], wv[:], ident[:])
            tr(F[:, 0, 320:336], b1n[:], ident[0:EXPERTS, 0:EXPERTS])
            tr(F[:, 0, 336:336 + LAYERS], bg_rows[:].rearrange("l b d -> l (b d)"), ident[0:LAYERS, 0:LAYERS]
               ).then_inc(s_turn, 1)
            for e in range(EXPERTS):
                t = tr(Z[:, e // 8, D * (e % 8):D * (e % 8 + 1)], w1n[:, e, :], ident[0:D, 0:D])
            t.then_inc(s_w1t, 1)
            pe.wait_ge(s_reach, 2)
            tr(F[0:1, 1, 0:EP], reach[:, EC:EC + 1], ident[0:EP, 0:EP]).then_inc(s_reachT, 1)
            pe.wait_ge(s_oned, 2)
            pe.wait_ge(s_hot, 2)
            for t in range(NB):
                for j in range(EC):
                    m = mm(F[0:TB, 2, t:t + 1], hot[:, 1, j, TB * t:TB * (t + 1)], one16[0:EP, :],
                           start=(j == 0), stop=(j == EC - 1))
            m.then_inc(s_degs, 1)
            pe.wait_ge(s_ddiag, 1)
            pe.wait_ge(s_wcopy, 3)
            pe.wait_ge(s_far, 1)
            for t in range(NB):
                h, o = t // 4, TB * (t % 4)
                m = mm(F[0:TB, h, o:o + TB], ones[:], ddiag[:, t, :], start=True, stop=True)
            m.then_inc(s_dinv_ps, 1)
            far_pe = pe.value_load(far[0:1, 0:1], min_val=0, max_val=1)
            pe.wait_ge(s_hot, 3)
            pe.wait_ge(s_dinv, 2)

            def count(q, t, n0, n1, inc):
                if q >= 4:
                    pe.wait_ge(s_adj, inc * (q - 3))
                for j in range(EC):
                    mm(F[0:TB, q % 4, 0:n1 - n0], hot[:, 0, j, TB * t:TB * (t + 1)], hot[:, 1, j, n0:n1],
                       start=(j == 0), stop=False)
                mm(F[0:TB, q % 4, 0:n1 - n0], self_hot[:, 0, 0:TB], self_hot[:, t, n0:n1], start=False, stop=True
                   ).then_inc(s_cnt, inc)

            with pe.If(far_pe):
                for q in range(2 * NB):
                    count(q, q // 2, HALF * (q % 2), HALF * (q % 2 + 1), 1)
            with pe.Else():
                for t in range(NB):
                    count(t, t, *window(t), 2)
            pe.wait_ge(s_w1c, 6)
            for part in range(2):
                for e in range(EXPERTS):
                    dst = (O if part == 0 else Z)[:, e // 8, :].bitcast(F16)
                    t = tr(dst[:, FF * (e % 8):FF * (e % 8 + 1)], w1T[:, part, e].rearrange("f u k -> f (u k)"),
                           ident16[:])
                t.then_inc(s_w1p, 1)

            def front_step(what, idx, p, par):
                if what == "embed":
                    if idx == 0:
                        after(pe, "x_in", p, 192)
                        after(pe, "tokens", p, 0)
                        if isinstance(p, int) and p == 0:
                            pe.wait_ge(s_adj, 2 * NB)
                    v = xt[:].rearrange("p i (j w) -> p i j w", w=PATCH)
                    for w in range(RUN):
                        m = mm(F[:, idx, 0:HALF], wemb[:, w, :], v[:, 14 * idx:14 * idx + 14, :, w],
                               start=(w == 0), stop=(w == RUN - 1))
                    m.then_inc(sems["embedded"], 1)
                elif what == "node_mix":
                    if idx == 0:
                        after(pe, "embed", p, 2)
                    else:
                        after(pe, "graph", p, 2 * idx)
                    for t in range(NB):
                        m = mm(F[0:TB, t // 4, 128 * (t % 4):128 * (t % 4 + 1)], H[:, TB * t:TB * (t + 1)],
                               wg[:, idx, :], start=True, stop=True)
                        if t in (3, 6):
                            m.then_inc(sems["mixed"], 1)
                elif what == "aggregate":
                    after(pe, "nodes", p, 2 * idx + 2)
                    with pe.If(far_pe):
                        for h in range(2):
                            for t in range(NB):
                                m = mm(F[:, h, 0:HALF], X[:, t, :], adj[:, t, HALF * h:HALF * (h + 1)],
                                       start=(t == 0), stop=(t == NB - 1))
                            m.then_inc(sems["aggregated"], 1)
                    with pe.Else():
                        for h in range(2):
                            near = [t for t in range(NB) if window(t)[0] < HALF * (h + 1) and window(t)[1] > HALF * h]
                            for t in near:
                                n0, n1 = max(window(t)[0], HALF * h), min(window(t)[1], HALF * (h + 1))
                                m = mm(F[:, h, n0 - HALF * h:n1 - HALF * h], X[:, t, :], adj[:, t, n0:n1],
                                       start=(t == near[0]), stop=(t == near[-1]), skip_group_check=True)
                            m.then_inc(sems["aggregated"], 1)
                elif what == "tokens":
                    after(pe, "graph", p, 6)
                    for c in range(NC):
                        n = TOK if c < NC - 1 else LASTIMG
                        m = mm(F[0:n, c // 4, 128 * (c % 4):128 * (c % 4 + 1)], H[:, TOK * c:TOK * c + n], wtok[:],
                               start=True, stop=True)
                        if c % 4 == 3:
                            m.then_inc(sems["tokens_ps"], 1)
                elif what == "x1_turn":
                    after(pe, "normed", p, 1)
                    for c in range(NC):
                        t = tr(F[:, 2 + c // 4, TOK * (c % 4):TOK * (c % 4 + 1)],
                               x1[:, c].rearrange("p b d -> p (b d)"), ident[0:TOK, 0:TOK])
                        if c % 4 == 3:
                            t.then_inc(sems["x1_turned"], 1)
                elif what == "keys":
                    after(pe, "x1T_ready", p, 2)
                    for h in range(2):
                        m = mm(F[:, 2 + h, 0:GROUP], wk[:], x1T[:, 4 * h:4 * h + 4, :].rearrange("p c t -> p (c t)"),
                               start=True, stop=True)
                    m.then_inc(sems["keys_ps"], 1)
                elif what == "keys_turn":
                    after(pe, "kexp", p, 1)
                    for c in range(NC):
                        t = tr(F[0:TOK, 2 + c // 4, 128 * (c % 4):128 * (c % 4 + 1)], ET[:, c, :], ident[:])
                        if c % 4 == 3:
                            t.then_inc(sems["keys_turned"], 1)
                elif what == "kx":
                    after(pe, "keys_ready", p, 2)
                    for c in range(NC):
                        m = mm(F[:, 2, 0:128], x1[:, c].rearrange("p b d -> p (b d)"), Ek[:, c, :],
                               start=(c == 0), stop=(c == NC - 1))
                    m.then_inc(sems["kx_ps"], 1)
                elif what == "kq":
                    after(pe, "kx_ready", p, 1)
                    mm(F[:, 3, 0:128], kx[:], wq[:], start=True, stop=True).then_inc(sems["kq_ps"], 1)
                elif what == "vkq":
                    after(pe, "kq_ready", p, 2)
                    mm(F[:, 2, 0:128], wvT[:], kq[:], start=True, stop=True).then_inc(sems["vkq_ps"], 1)
                elif what == "heads":
                    after(pe, "vkq_ready", p, 1)
                    xs = x1T[:].rearrange("p c t -> p (c t)").rearrange("p (m t) -> p t m", t=NC)
                    for t in range(NC):
                        m = mm(F[0:TOK, 2 + t // 4, 128 * (t % 4):128 * (t % 4 + 1)], xs[:, t, :], vkq[:],
                               start=True, stop=True)
                        if t % 4 == 3:
                            m.then_inc(sems["heads_ps"], 1)
                elif what == "heads_turn":
                    after(pe, "heads_a", p, 1)
                    after(pe, "heads_b", p, 1)
                    for hp in range(HEADS):
                        t = tr(F[:, 2 + hp // 4, TOK * (hp % 4):TOK * (hp % 4 + 1)],
                               zh[:, 2 * hp:2 * hp + 2].rearrange("p h t e -> p (h t e)"), ident[0:TOK, 0:TOK])
                        if hp % 4 == 3:
                            t.then_inc(sems["heads_turned"], 1)
                elif what == "attn_out":
                    after(pe, "zT_ready", p, 2)
                    for hp in range(HEADS):
                        m = mm(F[0:TOK, 2 + hp // 4, 128 * (hp % 4):128 * (hp % 4 + 1)], zT[:, hp, :], watt[:],
                               start=True, stop=True)
                        if hp % 4 == 3:
                            m.then_inc(sems["attn_ps"], 1)
                elif what == "x2_turn":
                    after(pe, "x2_parts", p, 2)
                    for b in range(2):
                        for c in range(NC):
                            t = tr(bank16(2 + b)[:, TOK * c:TOK * (c + 1)], x2s[:, c, b].rearrange("p u d -> p (u d)"),
                                   ident16[0:TOK, 0:TOK])
                        t.then_inc(sems["x2_turned"], 1)
                elif what == "logits":
                    after(pe, "x2T_ready", p, 2)
                    if isinstance(p, int) and p == 0:
                        pe.wait_ge(s_gw, 6)
                    for b in range(2):
                        for c in range(NC):
                            m = mm(F[0:TOK, 2 + b, 48 * c:48 * (c + 1)], x2T[:, par, b, TOK * c:TOK * (c + 1)],
                                   gw3[:].rearrange("p u e -> p (u e)"), start=True, stop=True)
                        m.then_inc(sems["logits_ps"], 1)
                elif what == "gates_turn":
                    after(pe, "gates", p, 4)
                    for b in range(2):
                        t = tr(F[:, 2, TOK * b:TOK * (b + 1)],
                               gate[:, par, NC * b:NC * (b + 1), :].rearrange("p c e -> p (c e)"), ident[0:TOK, 0:TOK])
                    t.then_inc(sems["gates_turned"], 1)
                elif what == "bias2":
                    after(pe, "gates_ready", p, 1)
                    for b in range(2):
                        mm(F[0:TOK, 2 + b, :], gT[:, b, :], b2d[:].rearrange("p c d -> p (c d)"),
                           start=True, stop=True).then_inc(sems["bias2_ps"], 1)

            def hidden(p, par, n):
                g, e = divmod(n, EXPERTS)
                if n == 0:
                    after(pe, "x2T_ready", p, 2)
                    if isinstance(p, int) and p == 0:
                        pe.wait_ge(s_w1s, 2)
                after(pe, "hidden", p, n - 1)
                for part in range(2):
                    m = mm(Z[:, n % 2, 0:GROUP], w1s[:, part, e, :],
                           x2T[:, par, g // 2, GROUP * (g % 2):GROUP * (g % 2 + 1)],
                           start=(part == 0), stop=(part == 1))
                m.then_inc(sems["hidden_ps"], 1)

            def ffn_step(p, par, n):
                if n == 0:
                    hidden(p, par, 0)
                    hidden(p, par, 1)
                if n + 2 < STEPS:
                    hidden(p, par, n + 2)
                u = n // 2
                if n % 2 == 0:
                    after(pe, "gated", p, u - 1)
                after(pe, "hidden", p, n + 1)
                for c in range(4):
                    m = mm(O[0:TOK, u % 2, 128 * c + D * (n % 2):128 * c + D * (n % 2 + 1)],
                           hid[:, n % 4, TOK * c:TOK * (c + 1)], w2s[:, n % EXPERTS, :], start=True, stop=True)
                if n % 2:
                    m.then_inc(sems["outputs_ps"], 1)

            run(pe, "pe", front_step, ffn_step, None)

        @block.scalar
        def _(act):
            act.wait_ge(s_w1p, 1)
            act.copy(w1s[:, 0].rearrange("p (h e) f -> p h (e f)", h=2), O[:].bitcast(F16)).then_inc(s_w1s, 1)
            act.wait_ge(s_w1p, 2)
            act.copy(w1s[:, 1].rearrange("p (h e) f -> p h (e f)", h=2), Z[:].bitcast(F16)).then_inc(s_w1s, 1)
            act.wait_ge(s_wcopy, 3)

            def front_step(what, idx, p, par):
                if what == "graph_relu":
                    for h in range(2):
                        after(act, "aggregated", p, 2 * idx + h + 1)
                        act.activation(H[:, HALF * h:HALF * (h + 1)], F[:, h, 0:HALF], ACT.Relu,
                                       bias=bg[:, idx:idx + 1]).then_inc(sems["graph"], 1)
                elif what == "ln_square":
                    after(act, "centred", p, idx + 1)
                    act.activation(sq[:], xc[:], ACT.Square).then_inc(sems["squared"], 1)
                elif what == "x1_copy":
                    for h in range(2):
                        after(act, "x1_turned", p, h + 1)
                        act.copy(x1T[:, 4 * h:4 * h + 4, :].rearrange("p c t -> p (c t)"), F[:, 2 + h, 0:GROUP]
                                 ).then_inc(sems["x1T_ready"], 1)
                elif what == "keys_exp":
                    after(act, "kmax", p, 1)
                    act.activation(ET[:].rearrange("p (h c) t -> p h (c t)", h=2), F[:, 2:4, 0:GROUP], ACT.Exp,
                                   bias=kneg[:], accum_out=ksum[:]).then_inc(sems["kexp"], 1)
                elif what == "heads_copy":
                    after(act, "heads_ps", p, 2)
                    act.copy(zh[:, :, 4:8, :].rearrange("p h t e -> p t h e"),
                             F[0:TOK, 3, :].rearrange("p (t h e) -> p t h e", t=4, e=DH)).then_inc(sems["heads_b"], 1)
                elif what == "heads_turned":
                    for h in range(2):
                        after(act, "heads_turned", p, h + 1)
                        act.copy(zT[:, 4 * h:4 * h + 4, :].rearrange("p c t -> p (c t)"), F[:, 2 + h, 0:GROUP]
                                 ).then_inc(sems["zT_ready"], 1)
                elif what == "x2_copy":
                    for b in range(2):
                        after(act, "x2_turned", p, b + 1)
                        act.copy(x2T[:, par, b, :], bank16(2 + b)[:, 0:SEQ]).then_inc(sems["x2T_ready"], 1)
                elif what == "top2_exp":
                    after(act, "top2", p, 10)
                    act.activation(tv[:, 5], tv[:, 4], ACT.Exp).then_inc(sems["top2_exp"], 1)

            def ffn_step(p, par, n):
                after(act, "hidden_ps", p, n + 1)
                after(act, "outputs_ps", p, n // 2 - 1)
                act.activation(hid[:, n % 4, :], Z[:, n % 2, 0:GROUP], ACT.Relu,
                               bias=b1s[:, n % EXPERTS:n % EXPERTS + 1]).then_inc(sems["hidden"], 1)

            def final_step(what, p, par, b):
                if what == "f_square":
                    after(act, "f_centred", p, b + 1)
                    after(act, "stored", p, 0)
                    act.activation(fin[:, b], fxc[:], ACT.Square).then_inc(sems["f_squared"], 1)

            run(act, "act", front_step, ffn_step, final_step)

        @block.vector
        def _(dve):
            tt, ts, cp = dve.tensor_tensor, dve.tensor_scalar, dve.tensor_copy
            dve.wait_ge(s_edge, 16)
            cp(ef[:], eidx[:]).then_inc(s_ef, 1)
            dve.wait_ge(s_const, 80)
            cp(iota16[:], iota).then_inc(s_ef, 1)
            cp(ident16[:], ident[:]).then_inc(s_ef, 1)
            dve.wait_ge(s_ef, 3)
            tt(reach[:, 0:EC], ef[:, 0, :], ef[:, 1, :], ALU.subtract).then_inc(s_reach, 1)
            dve.wait_ge(s_reach, 1)
            dve.tensor_reduce(reach[:, EC:EC + 1], reach[:, 0:EC], AX.X, ALU.max, apply_absolute_value=True
                              ).then_inc(s_reach, 1)
            for a in (1, 0):
                for j in range(EC):
                    m = ts(hot[:, a, j, :], iota16[0:EP, :], ef[:, a, j:j + 1], None, ALU.is_equal)
                m.then_inc(s_hot, 1)
            for t in range(NB):
                m = ts(self_hot[:, t, :], iota16[0:TB, :], node[:, t:t + 1], None, ALU.is_equal)
            m.then_inc(s_hot, 1)
            dve.wait_ge(s_reachT, 1)
            dve.tensor_reduce(far_max[:], F[0:1, 1, 0:EP], AX.X, ALU.max).then_inc(s_reach, 1)
            dve.wait_ge(s_reach, 3)
            ts(far[:], far_max[:], float(REACH), None, ALU.is_gt).then_inc(s_far, 1)
            dve.wait_ge(s_turn, 1)
            cp(wvT[:], F[:, 0, 192:320]).then_inc(s_wcopy, 1)
            cp(bg[:], F[:, 0, 336:336 + LAYERS]).then_inc(s_wcopy, 1)
            ts(pos[:], pos[:], bemb[:], None, ALU.add).then_inc(s_posb, 1)
            dve.wait_ge(s_w1t, 1)
            for h in range(2):
                dve.tensor_reduce(w1max[:, 8 * h:8 * h + 8], Z[:, h, :].rearrange("p (e k) -> p e k", k=D), AX.X,
                                  ALU.max, apply_absolute_value=True).then_inc(s_w1c, 1)
            dve.wait_ge(s_w1c, 2)
            ts(w1max[:], w1max[:], TINY, None, ALU.max).then_inc(s_w1c, 1)
            dve.wait_ge(s_w1c, 3)
            ts(w1pow[:].bitcast(I32), w1max[:].bitcast(I32), 0x7F800000, None, ALU.bitwise_and).then_inc(s_w1c, 1)
            dve.wait_ge(s_w1c, 4)
            dve.reciprocal(w1inv[:], w1pow[:]).then_inc(s_inv, 1)
            dve.wait_ge(s_inv, 1)
            tt(b1s[:], F[:, 0, 320:336], w1inv[:], ALU.mult).then_inc(s_wcopy, 1)
            for h in range(2):
                m = tt(w1sc[:, 8 * h:8 * h + 8, :], Z[:, h, :].rearrange("p (e k) -> p e k", k=D),
                       bc(w1inv[:, 8 * h:8 * h + 8], D), ALU.mult)
            m.then_inc(s_w1c, 1)
            tt(w2s[:], w2s[:], bc(w1pow[:], D), ALU.mult)
            dve.wait_ge(s_w1c, 5)
            for u in range(2):
                m = cp(w1T[:, 0, :, u, :], w1sc[:])
            m.then_inc(s_gw, 1)
            dve.wait_ge(s_gw, 1)
            for u in range(2):
                m = tt(w1T[:, 1, :, u, :], w1sc[:], w1T[:, 0, :, u, :], ALU.subtract)
            m.then_inc(s_w1c, 1)
            cp(gw3[:, 0, :], gw[:]).then_inc(s_gw, 1)
            dve.wait_ge(s_gw, 2)
            tt(gwr[:, 0, :], gw[:], gw3[:, 0, :], ALU.subtract).then_inc(s_gw, 1)
            dve.wait_ge(s_gw, 3)
            cp(gw3[:, 1, :], gwr[:, 0, :]).then_inc(s_gw, 1)
            dve.wait_ge(s_gw, 4)
            tt(gwr[:, 1, :], gwr[:, 0, :], gw3[:, 1, :], ALU.subtract).then_inc(s_gw, 1)
            dve.wait_ge(s_gw, 5)
            cp(gw3[:, 2, :], gwr[:, 1, :]).then_inc(s_gw, 1)
            dve.wait_ge(s_degs, 1)
            ts(degc[:], F[0:TB, 2, 0:NB], 1.0, None, ALU.add).then_inc(s_deg, 1)
            dve.wait_ge(s_dsrc, 1)
            for t in range(NB):
                m = ts(ddiag[:, t, :], ident[0:TB, 0:TB], dsrc[:, t:t + 1], None, ALU.mult)
            m.then_inc(s_ddiag, 1)
            dve.wait_ge(s_dinv_ps, 1)
            cp(dinv[:, 0:4 * TB], F[0:TB, 0, 0:4 * TB]).then_inc(s_dinv, 1)
            cp(dinv[:, 4 * TB:], F[0:TB, 1, 0:3 * TB]).then_inc(s_dinv, 1)
            far_dve = dve.value_load(far[0:1, 0:1], min_val=0, max_val=1)
            dve.wait_ge(s_dinv, 2)

            def weigh(q, t, n0, n1, inc):
                dve.wait_ge(s_cnt, inc * (q + 1))
                dve.scalar_tensor_tensor(adj[:, t, n0:n1], F[0:TB, q % 4, 0:n1 - n0], dsrc[:, t:t + 1],
                                         dinv[:, n0:n1], ALU.mult, ALU.mult).then_inc(s_adj, inc)

            with dve.If(far_dve):
                for q in range(2 * NB):
                    weigh(q, q // 2, HALF * (q % 2), HALF * (q % 2 + 1), 1)
            with dve.Else():
                for t in range(NB):
                    weigh(t, t, *window(t), 2)

            def ln_center(src, dst_c, stats, groups, p, k, pre):
                base_n = 3 * k
                dve.tensor_reduce(stats[:, 0, 0:groups], src, AX.X, ALU.add).then_inc(sems[pre + "stat"], 1)
                after(dve, pre + "stat", p, base_n + 1)
                ts(stats[:, 1, 0:groups], stats[:, 0, 0:groups], -1.0 / D, None, ALU.mult
                   ).then_inc(sems[pre + "stat"], 1)
                after(dve, pre + "stat", p, base_n + 2)
                tt(dst_c, src, bc(stats[:, 1, 0:groups], D), ALU.add).then_inc(sems[pre + "centred"], 1)

            def ln_var(sqv, stats, groups, p, k, pre):
                after(dve, pre + "squared", p, k + 1)
                dve.tensor_reduce(stats[:, 2, 0:groups], sqv, AX.X, ALU.add).then_inc(sems[pre + "stat"], 1)
                after(dve, pre + "stat", p, 3 * k + 3)
                ts(stats[:, 3, 0:groups], stats[:, 2, 0:groups], 1.0 / D, EPS, ALU.mult, ALU.add
                   ).then_inc(sems[pre + "variance"], 1)

            def front_step(what, idx, p, par):
                if what == "embed_copy":
                    for h in range(2):
                        after(dve, "embedded", p, h + 1)
                        if h == 0:
                            after(dve, "tokens_ps", p, 0)
                            if isinstance(p, int) and p == 0:
                                dve.wait_ge(s_posb, 1)
                        n = slice(HALF * h, HALF * (h + 1))
                        tt(H[:, n], F[:, h, 0:HALF], pos[:, n], ALU.add).then_inc(sems["embed"], 1)
                elif what == "node_copy":
                    for h, (t0, t1) in enumerate(((0, 4), (4, 7))):
                        after(dve, "mixed", p, 2 * idx + h + 1)
                        if h == 0:
                            after(dve, "aggregated", p, 2 * idx)
                        cp(X[:, t0:t1, :].rearrange("p t f -> p (t f)"), F[0:TB, h, 0:128 * (t1 - t0)]
                           ).then_inc(sems["nodes"], 1)
                elif what == "tokens_copy":
                    after(dve, "tokens_ps", p, 2)
                    after(dve, "hbeta", p, 0)
                    after(dve, "centred", p, 1 - 3)
                    after(dve, "txt_in", p, 32)
                    bt = rows(btok[:], 8)
                    tt(flat(hL[:, 0:4]), F[0:TOK, 0, :].rearrange("p (c d) -> p c d", d=D), bt, ALU.add
                       ).then_inc(sems["tokens"], 1)
                    tt(flat(hL[:, 4:7]), F[0:TOK, 1, 0:384].rearrange("p (c d) -> p c d", d=D), bt[:, 0:6], ALU.add
                       ).then_inc(sems["tokens"], 1)
                    tt(hL[0:LASTIMG, 7], F[0:LASTIMG, 1, 384:512].rearrange("p (c d) -> p c d", d=D),
                       bt[0:LASTIMG, 0:2], ALU.add).then_inc(sems["tokens"], 1)
                elif what == "ln_center":
                    if idx == 0:
                        after(dve, "tokens", p, 3)
                        src = flat(hL[:])
                    elif idx == 1:
                        after(dve, "attn", p, 2)
                        src = flat(yL[:])
                    else:
                        after(dve, "hres", p, 1)
                        src = flat(hres[:, par])
                    ln_center(src, xc[:], st[:, idx], 2 * NC, p, idx, "")
                elif what == "ln_var":
                    ln_var(sq[:], st[:, idx], 2 * NC, p, idx, "")
                elif what == "ln_apply":
                    after(dve, "rstd", p, idx + 1)
                    if idx == 2:
                        after(dve, "summed", p - 2, 4)
                    dst = (flat(x1[:]), flat(yn[:]), flat(x2[:, par]))[idx]
                    tt(dst, xc[:], bc(st[:, idx, 4], D), ALU.mult).then_inc(sems["normed"], 1)
                elif what == "keys_max":
                    after(dve, "keys_ps", p, 1)
                    dve.tensor_reduce(kneg[:], F[:, 2:4, 0:GROUP], AX.XY, ALU.max, negate=True
                                      ).then_inc(sems["kmax"], 1)
                elif what == "keys_copy":
                    for h in range(2):
                        after(dve, "keys_turned", p, h + 1)
                        cp(Ek[:, 4 * h:4 * h + 4, :].rearrange("p c f -> p (c f)"), F[0:TOK, 2 + h, :]
                           ).then_inc(sems["keys_ready"], 1)
                elif what == "kx_copy":
                    after(dve, "kx_ps", p, 1)
                    cp(kx[:], F[:, 2, 0:128]).then_inc(sems["kx_ready"], 1)
                elif what == "kq_mask":
                    dve.reciprocal(kinv[:], ksum[:]).then_inc(sems["kq_ready"], 1)
                    after(dve, "kq_ready", p, 1)
                    after(dve, "kq_ps", p, 1)
                    dve.scalar_tensor_tensor(kq[:], F[:, 3, 0:128], kinv[:], mask[:], ALU.mult, ALU.mult
                                             ).then_inc(sems["kq_ready"], 1)
                elif what == "vkq_copy":
                    after(dve, "vkq_ps", p, 1)
                    cp(vkq[:], F[:, 2, 0:128]).then_inc(sems["vkq_ready"], 1)
                elif what == "heads_copy":
                    after(dve, "heads_ps", p, 1)
                    cp(zh[:, :, 0:4, :].rearrange("p h t e -> p t h e"),
                       F[0:TOK, 2, :].rearrange("p (t h e) -> p t h e", t=4, e=DH)).then_inc(sems["heads_a"], 1)
                elif what == "attn_bias":
                    for b in range(2):
                        after(dve, "attn_ps", p, b + 1)
                        tt(yL[:, :, b, :], F[0:TOK, 2 + b, :].rearrange("p (c d) -> p c d", d=D), rows(batt[:], NC),
                           ALU.add).then_inc(sems["attn"], 1)
                elif what == "residual":
                    after(dve, "normed", p, 2)
                    tt(flat(yn[:]), flat(yn[:]), rows(ga_b[:], 2 * NC), ALU.mult).then_inc(sems["gam"], 1)
                    after(dve, "gam", p, 1)
                    after(dve, "hbeta", p, 1)
                    after(dve, "final", p - 2, 2)
                    tt(flat(hres[:, par]), flat(yn[:]), flat(hb[:]), ALU.add).then_inc(sems["hres"], 1)
                elif what == "x2_split":
                    after(dve, "normed", p, 3)
                    v = x2[:, par]
                    cp(x2s[:, :, :, 0, :], v).then_inc(sems["x2_parts"], 1)
                    after(dve, "x2_parts", p, 1)
                    tt(x2s[:, :, :, 1, :], v, x2s[:, :, :, 0, :], ALU.subtract).then_inc(sems["x2_parts"], 1)
                elif what == "top2_a":
                    for b in range(2):
                        after(dve, "logits_ps", p, b + 1)
                        dve.tensor_reduce(lg[:, NC * b:NC * (b + 1), :],
                                          F[0:TOK, 2 + b, 0:48 * NC].rearrange("p (c u e) -> p c e u", u=3, e=EXPERTS),
                                          AX.X, ALU.add).then_inc(sems["top2"], 1)
                    after(dve, "top2", p, 2)
                    tt(lg[:], lg[:], rows(gateb[:], 2 * NC), ALU.add).then_inc(sems["top2"], 1)
                    after(dve, "top2", p, 3)
                    top(lg, 0, p, 3)
                elif what == "top2_b":
                    dve.scalar_tensor_tensor(lg2[:], ohot[:, 0], -HUGE, lg[:], ALU.mult, ALU.add
                                             ).then_inc(sems["top2"], 1)
                    after(dve, "top2", p, 8)
                    dve.tensor_reduce(tv[:, 1], lg2[:], AX.X, ALU.max).then_inc(sems["top2"], 1)
                    after(dve, "top2", p, 9)
                    tt(tv[:, 4], tv[:, 1], tv[:, 0], ALU.subtract).then_inc(sems["top2"], 1)
                    tt(hit[:, 1], lg2[:], bc(tv[:, 1], EXPERTS), ALU.is_equal).then_inc(sems["top2"], 1)
                    after(dve, "top2", p, 11)
                    tt(hit[:, 1], hit[:, 1], rows(rev[:], 2 * NC), ALU.mult).then_inc(sems["top2"], 1)
                    after(dve, "top2", p, 12)
                    dve.tensor_reduce(tv[:, 3], hit[:, 1], AX.X, ALU.max).then_inc(sems["top2"], 1)
                    after(dve, "top2", p, 13)
                    tt(ohot[:, 1], hit[:, 1], bc(tv[:, 3], EXPERTS), ALU.is_equal).then_inc(sems["top2"], 1)
                elif what == "top2_c":
                    after(dve, "top2_exp", p, 1)
                    ts(tv[:, 6], tv[:, 5], 1.0, None, ALU.add).then_inc(sems["top2"], 1)
                    after(dve, "top2", p, 15)
                    dve.reciprocal(tv[:, 7], tv[:, 6]).then_inc(sems["top2"], 1)
                    after(dve, "top2", p, 16)
                    tt(tv[:, 8], tv[:, 5], tv[:, 7], ALU.mult).then_inc(sems["gates"], 1)
                    tt(hit[:, 0], ohot[:, 0], bc(tv[:, 7], EXPERTS), ALU.mult).then_inc(sems["gates"], 1)
                    after(dve, "gates", p, 2)
                    tt(hit[:, 1], ohot[:, 1], bc(tv[:, 8], EXPERTS), ALU.mult).then_inc(sems["gates"], 1)
                    after(dve, "gates", p, 3)
                    tt(gate[:, par], hit[:, 0], hit[:, 1], ALU.add).then_inc(sems["gates"], 1)
                elif what == "gates_copy":
                    after(dve, "gates_turned", p, 1)
                    cp(gT[:].rearrange("p b t -> p (b t)"), F[:, 2, 0:2 * TOK]).then_inc(sems["gates_ready"], 1)
                elif what == "base":
                    for b in range(2):
                        after(dve, "bias2_ps", p, b + 1)
                        tt(base[:, par, b], x2[:, par, :, b, :], F[0:TOK, 2 + b, :].rearrange("p (c d) -> p c d", d=D),
                           ALU.add).then_inc(sems["base"], 1)

            def top(src, k, p, n0):
                dve.tensor_reduce(tv[:, k], src[:], AX.X, ALU.max).then_inc(sems["top2"], 1)
                after(dve, "top2", p, n0 + 1)
                tt(hit[:, k], src[:], bc(tv[:, k], EXPERTS), ALU.is_equal).then_inc(sems["top2"], 1)
                after(dve, "top2", p, n0 + 2)
                tt(hit[:, k], hit[:, k], rows(rev[:], 2 * NC), ALU.mult).then_inc(sems["top2"], 1)
                after(dve, "top2", p, n0 + 3)
                dve.tensor_reduce(tv[:, 2 + k], hit[:, k], AX.X, ALU.max).then_inc(sems["top2b"], 1)
                after(dve, "top2b", p, 1)
                tt(ohot[:, k], hit[:, k], bc(tv[:, 2 + k], EXPERTS), ALU.is_equal).then_inc(sems["top2"], 1)
                after(dve, "top2", p, n0 + 4)

            def ffn_step(p, par, n):
                if n % 2 == 1:
                    u = n // 2
                    g, ep = divmod(u, 8)
                    after(dve, "outputs_ps", p, u + 1)
                    gv = gate[:, par, 4 * g:4 * g + 4, 2 * ep:2 * ep + 2]
                    gv = gv.unsqueeze(3).to_broadcast([TOK, 4, 2, D])
                    src = O[0:TOK, u % 2, :].rearrange("p (c e d) -> p c e d", c=4, e=2)
                    if ep == 0:
                        after(dve, "folded", p, g - 1)
                        dst = acc[:, g % 2]
                    else:
                        after(dve, "added", p, 7 * g + ep - TMPS)
                        dst = tmp[:, (7 * g + ep) % TMPS].rearrange("p (c e d) -> p c e d", c=4, e=2)
                    tt(dst, src, gv, ALU.mult).then_inc(sems["gated"], 1)

            def final_step(what, p, par, b):
                if what == "f_center":
                    after(dve, "summed", p, 2 * b + 2)
                    ln_center(ys[:], fxc[:], fst, NC, p, b, "f_")
                elif what == "f_var":
                    ln_var(fin[:, b], fst, NC, p, b, "f_")
                elif what == "f_apply":
                    after(dve, "f_rstd", p, b + 1)
                    tt(fxc[:], fxc[:], bc(fst[:, 4, 0:NC], D), ALU.mult).then_inc(sems["f_normed"], 1)

            run(dve, "dve", front_step, ffn_step, final_step)

        @block.gpsimd
        def _(pool):
            tt = pool.tensor_tensor
            for w in (wemb, wg, wtok, wk, wq, wv, watt, b2d):
                m = pool.memset(w[:], 0.0)
            m.then_inc(s_wz, 1)
            pool.memset(one16[:], 1.0).then_inc(s_oned, 1)
            pool.memset(ones[:], 1.0).then_inc(s_oned, 1)
            pool.memset(mhalf[:], -0.5).then_inc(s_half, 1)
            for e in range(EXPERTS):
                m = pool.memset(rev[:, e:e + 1], float(EXPERTS - e))
            m.then_inc(s_half, 1)
            pool.wait_ge(s_half, 2)
            pool.wait_ge(s_deg, 1)
            tt(dsrc[:], degc[:], mhalf[0:TB, 0:NB], ALU.pow).then_inc(s_dsrc, 1)
            pool.wait_ge(s_w, 16 * NW)

            def front_step(what, idx, p, par):
                if what == "ln_rstd":
                    after(pool, "variance", p, idx + 1)
                    tt(st[:, idx, 4], st[:, idx, 3], mhalf[0:TOK, 0:2 * NC], ALU.pow).then_inc(sems["rstd"], 1)
                    if idx == 0:
                        after(pool, "hres", p, 0)
                        tt(flat(hb[:]), flat(hL[:]), rows(ba_b[:], 2 * NC), ALU.add).then_inc(sems["hbeta"], 1)

            def ffn_step(p, par, n):
                if n % 2 == 1:
                    u = n // 2
                    g, ep = divmod(u, 8)
                    if ep:
                        a = acc[:, g % 2].rearrange("p c e d -> p (c e d)")
                        after(pool, "gated", p, u + 1)
                        after(pool, "added", p, 7 * g + ep - 1)
                        tt(a, a, tmp[:, (7 * g + ep) % TMPS], ALU.add).then_inc(sems["added"], 1)
                    if ep == 7:
                        b, h = g // 2, g % 2
                        after(pool, "added", p, 7 * (g + 1))
                        if h == 0:
                            after(pool, "f_centred", p, b)
                        dst = ys[:, 4 * h:4 * h + 4, :]
                        tt(dst, acc[:, g % 2, :, 0, :], acc[:, g % 2, :, 1, :], ALU.add).then_inc(sems["folded"], 1)
                        after(pool, "folded", p, g + 1)
                        tt(dst, dst, base[:, par, b, 4 * h:4 * h + 4, :], ALU.add).then_inc(sems["summed"], 1)

            def final_step(what, p, par, b):
                if what == "f_rstd":
                    after(pool, "f_variance", p, b + 1)
                    tt(fst[:, 4, 0:NC], fst[:, 3, 0:NC], mhalf[0:TOK, 0:NC], ALU.pow).then_inc(sems["f_rstd"], 1)
                elif what == "f_gamma":
                    after(pool, "f_normed", p, b + 1)
                    tt(fxc[:], fxc[:], rows(gf_b[:], NC), ALU.mult).then_inc(sems["f_gamma"], 1)
                elif what == "f_beta":
                    after(pool, "f_gamma", p, b + 1)
                    tt(fxc[:], fxc[:], rows(bf_b[:], NC), ALU.add).then_inc(sems["f_beta"], 1)
                elif what == "f_residual":
                    after(pool, "f_beta", p, b + 1)
                    tt(fin[:, b], fxc[:], hres[:, par, :, b, :], ALU.add).then_inc(sems["final"], 1)

            run(pool, "pool", front_step, ffn_step, final_step)


def constants():
    pos = np.arange(NODES, dtype=np.float32)[:, None]
    div = np.exp(np.arange(0, D, 2, dtype=np.float32) * np.float32(-math.log(10000.0) / D))
    pe = np.zeros((NODES, D), np.float32)
    pe[:, 0::2] = np.sin(pos * div)
    pe[:, 1::2] = np.cos(pos * div)
    head = np.arange(128) // DH
    return {
        "ident": np.eye(128, dtype=np.float32),
        "iota": np.broadcast_to(np.arange(NODES, dtype=np.float32), (128, NODES)).copy(),
        "node": (np.arange(TB)[:, None] + TB * np.arange(NB)[None, :]).astype(np.float32),
        "mask": ((head[:, None] == head[None, :]) * SCALE).astype(np.float32),
        "pos": np.concatenate([pe.T, pe.T]),
    }


_INS = ["x", "txt", "L0_tok_W_embed", "L0_tok_b_embed", "L0_tok_W_gcn", "L0_tok_b_gcn", "L0_tok_W_out",
        "L0_tok_b_out", "L0_tok_edge_index", "L0_attn_Wqkv", "L0_attn_Wout", "L0_attn_bout", "L0_attn_gamma",
        "L0_attn_beta", "L0_ffn_gate_w", "L0_ffn_gate_b", "L0_ffn_w1", "L0_ffn_b1", "L0_ffn_w2", "L0_ffn_b2",
        "L0_ffn_gamma", "L0_ffn_beta"]


def kernel(**inputs):
    import concourse.bacc as _bacc
    from concourse.bass_utils import run_bass_kernel_spmd as _run

    nc = _bacc.Bacc("TRN2", target_bir_lowering=False, num_devices=1)
    arrays, args = {}, []
    for name in _INS:
        a = np.ascontiguousarray(inputs[name])
        arrays["in_" + name] = a
        args.append(nc.dram_tensor("in_" + name, a.shape, mybir.dt.from_np(a.dtype), kind="ExternalInput").ap())
    for name, a in constants().items():
        arrays["const_" + name] = a
        args.append(nc.dram_tensor("const_" + name, a.shape, mybir.dt.from_np(a.dtype), kind="ExternalInput").ap())
    out = nc.dram_tensor("out_0", (IMAGES, SEQ, D), F32, kind="ExternalOutput").ap()
    build(nc, *args, out)
    r = _run(nc, [arrays], core_ids=[0])
    return r.results[0]["out_0"]
```

```python
from contextlib import ExitStack
import math

import numpy as np

import concourse.bass as bass
from concourse import mybir
from concourse.alu_op_type import AluOpType as ALU

ACT = mybir.ActivationFunctionType
AX = mybir.AxisListType
F32 = mybir.dt.float32
F16 = mybir.dt.float16
BF16 = mybir.dt.bfloat16
I32 = mybir.dt.int32

GRID, PATCH, CH = 28, 8, 3
NODES = GRID * GRID
D = 64
TXT = 32
SEQ = NODES + TXT
IMAGES = 16
PAIRS = IMAGES // 2
HEADS, DH = 8, 8
TB = 112
NB = NODES // TB
TOK = SEQ // HEADS
NC = SEQ // TOK
LASTIMG = NODES - (NC - 1) * TOK
HALF = NODES // 2
RUN = PATCH // 2
KE = 2 * 2 * CH * PATCH
LAYERS = 3
EXPERTS, FF = 16, 128
GROUP = 4 * TOK
TMPS = 3
STEPS = 4 * EXPERTS
UNITS = STEPS // 2
REACH = GRID
EPS = 1e-5
SCALE = float(D) ** -0.5
TINY = 2.0 ** -60
HUGE = 3.0e38


def window(t):
    return max(0, TB * t - REACH), min(NODES, TB * (t + 1) + REACH)


GRAPH = (
    ("embed", "pe", 0, 0), ("embed", "pe", 1, 5), ("node_copy", "dve", 0, 8), ("aggregate", "pe", 0, 14),
    ("graph_relu", "act", 0, 22), ("node_mix", "pe", 1, 24), ("node_copy", "dve", 1, 25),
    ("aggregate", "pe", 1, 30), ("graph_relu", "act", 1, 35), ("node_mix", "pe", 2, 37),
    ("node_copy", "dve", 2, 43), ("aggregate", "pe", 2, 49), ("graph_relu", "act", 2, 54),
    ("tokens", "pe", 0, 58), ("tokens_copy", "dve", 0, 58),
)
ATTENTION = (
    ("ln_sum", "dve", 0, 0), ("ln_sub", "dve", 0, 0), ("ln_square", "act", 0, 2), ("ln_var", "dve", 0, 2),
    ("ln_rstd", "pool", 0, 2), ("ln_apply", "dve", 0, 5), ("x1_turn", "pe", 0, 7), ("x1_copy", "act", 0, 9),
    ("keys", "pe", 0, 10), ("keys_max", "dve", 0, 10), ("keys_exp", "act", 0, 14), ("keys_turn", "pe", 0, 14),
    ("keys_copy", "dve", 0, 14), ("kx", "pe", 0, 15), ("kx_copy", "dve", 0, 15), ("kq", "pe", 0, 16),
    ("kq_mask", "dve", 0, 16), ("vkq", "pe", 0, 17), ("vkq_copy", "dve", 0, 18), ("heads", "pe", 0, 19),
    ("heads_copy", "dve", 0, 19), ("heads_copy", "act", 1, 20), ("heads_turn", "pe", 0, 20),
    ("heads_turned", "act", 0, 22), ("attn_out", "pe", 0, 22), ("attn_bias", "dve", 0, 22),
    ("ln_square", "act", 1, 25), ("ln_var", "dve", 1, 25), ("ln_rstd", "pool", 1, 25),
    ("res_gamma", "dve", 0, 27), ("ln_apply", "dve", 1, 29), ("res_beta", "dve", 0, 29),
    ("ln_sum", "dve", 2, 31), ("ln_sub", "dve", 2, 34), ("ln_square", "act", 2, 38), ("ln_var", "dve", 2, 38),
    ("ln_rstd", "pool", 2, 38), ("ln_apply", "dve", 2, 42), ("x2_hi", "dve", 0, 42), ("x2_lo", "dve", 0, 43),
    ("x2_turn", "pe", 0, 46), ("x2_copy", "act", 0, 48), ("logits", "pe", 0, 48), ("top2_sum", "dve", 0, 48),
    ("top2_a", "dve", 0, 50), ("top2_b", "dve", 0, 51), ("top2_exp", "act", 0, 55), ("top2_c", "dve", 0, 56),
    ("top2_d", "dve", 0, 58), ("gates_turn", "pe", 0, 61), ("gates_copy", "dve", 0, 62), ("bias2", "pe", 0, 63),
    ("base", "dve", 0, 63), ("hbeta", "pool", 0, 0), ("f_beta", "pool", 0, 46),
)
FINAL_0 = (
    ("f_sum", "dve", 0, 36), ("f_sub", "dve", 0, 39), ("f_square", "act", 0, 43), ("f_var", "dve", 0, 45),
    ("f_rstd", "pool", 0, 45), ("f_gamma", "dve", 0, 48), ("f_apply", "dve", 0, 53),
    ("f_residual", "dve", 0, 60),
)
FINAL_1 = (
    ("f_sum", "dve", 1, 3), ("f_sub", "dve", 1, 11), ("f_square", "act", 1, 15), ("f_var", "dve", 1, 16),
    ("f_rstd", "pool", 1, 18), ("f_gamma", "dve", 1, 19), ("f_apply", "dve", 1, 22),
    ("f_residual", "dve", 1, 28),
)
WEIGHTS = (
    (("gate_parts", "dve", 0, 20), ("centre", "dve", 0, 35)),
    (("w1_turn", "pe", 0, 0), ("w1_max", "dve", 0, 2), ("w1_scale", "dve", 0, 4), ("w2_scale", "dve", 0, 7),
     ("w1_hi", "dve", 0, 21), ("w1_lo", "dve", 0, 37), ("w1_lo", "dve", 1, 43), ("w1_back", "pe", 0, 48),
     ("w1_out", "act", 0, 49), ("w1_back", "pe", 1, 51), ("w1_out", "act", 1, 58)),
)


def build(nc, x, txt, W_embed, b_embed, W_gcn, b_gcn, W_out, b_out, edges, Wqkv, Wout, bout, ga, ba,
          gate_w, gate_b, w1, b1, w2, b2, gf, bf, c_ident, c_iota, c_mask, c_pos, out):
    E = edges.shape[1]
    EP = 126
    EC = E // EP
    assert EP * EC == E

    with ExitStack() as ctx:
        def sb(name, shape, dt=F32):
            return ctx.enter_context(nc.sbuf_tensor(name, shape, dt))

        def sem(name):
            return ctx.enter_context(nc.semaphore(name))

        F = ctx.enter_context(nc.psum_tensor("front", [128, 4, 512], F32))
        Z = ctx.enter_context(nc.psum_tensor("hidden_ps", [128, 2, 512], F32))
        O = ctx.enter_context(nc.psum_tensor("expert_ps", [128, 2, 512], F32))

        ident = sb("ident", [128, 128])
        ident16 = sb("ident16", [128, 128], F16)
        iota16 = sb("iota16", [128, NODES], F16)
        identb = sb("identb", [TB, TB], BF16)
        mask = sb("mask", [128, 128])
        posx = sb("posx", [TB, NB, 2 * D])
        wemb = sb("wemb", [KE, RUN, 2 * D])
        bemb = sb("bemb", [128, 1])
        wg = sb("wg", [128, LAYERS, 128])
        wtok = sb("wtok", [128, 128])
        wk = sb("wk", [128, 128])
        wq = sb("wq", [128, 128])
        wv = sb("wv", [128, 128])
        wvT = sb("wvT", [128, 128])
        watt = sb("watt", [128, 128])
        wmean = sb("wmean", [128, 3])
        bg_rows = sb("bg_rows", [LAYERS, 2, D])
        bg = sb("bg", [128, LAYERS])
        btok = sb("btok", [TOK, D])
        batt = sb("batt", [TOK, D])
        ga_b = sb("ga_b", [TOK, D])
        ba_b = sb("ba_b", [TOK, D])
        gf_b = sb("gf_b", [TOK, D])
        bf_b = sb("bf_b", [TOK, D])
        gateb = sb("gateb", [TOK, EXPERTS])
        rev = sb("rev", [TOK, EXPERTS])
        mhalf = sb("mhalf", [128, 2 * NC])
        gw = sb("gw", [128, EXPERTS])
        gwr = sb("gwr", [128, 2, EXPERTS])
        gw3 = sb("gw3", [128, 3, EXPERTS], BF16)
        w1max = sb("w1max", [FF, EXPERTS])
        w1pow = sb("w1pow", [FF, EXPERTS])
        w1inv = sb("w1inv", [FF, EXPERTS])
        w1s = sb("w1s", [128, 2, EXPERTS, FF], F16)
        b1n = sb("b1n", [EXPERTS, FF])
        b1s = sb("b1s", [FF, EXPERTS])
        w2s = sb("w2s", [FF, EXPERTS, D])
        b2d = sb("b2d", [128, NC, D])
        adj = sb("adj", [TB, NB, NODES])
        eidx = sb("eidx", [EP, 2, EC], I32)
        ef = sb("ef", [EP, 2, EC])
        shared = [[sb("shared_0", [128, EC * NODES]), 0], [sb("shared_1", [128, 10216]), 0]]

        alone = []

        def carve(area, shape, dt=F32):
            n = int(np.prod(shape[1:])) * (4 if dt == F32 else 2) // 4
            v = area[0][0:shape[0], area[1]:area[1] + n]
            area[1] += n
            if dt != F32:
                v = v.bitcast(dt)
            names = "abcde"[:len(shape) - 1]
            return v.rearrange(f"p ({' '.join(names)}) -> p {' '.join(names)}", **dict(zip(names, shape[1:])))

        def over(shape, dt=F32):
            n = int(np.prod(shape[1:])) * (4 if dt == F32 else 2) // 4
            for area in shared:
                if area[1] + n <= area[0].shape[1]:
                    return carve(area, shape, dt)
            alone.append(sb(f"alone_{len(alone)}", shape, dt))
            return alone[-1]

        hot = carve(shared[0], [EP, 2, EC, NODES], BF16)
        w1n = carve(shared[1], [D, EXPERTS, FF])
        w1sc = carve(shared[1], [FF, EXPERTS, D])
        w1T = carve(shared[1], [FF, 2, EXPERTS, 2, D], F16)
        pos = carve(shared[1], [128, NODES])
        wembT = carve(shared[1], [128, RUN, KE])
        ddiag = carve(shared[1], [TB, NB, TB])
        iota = carve(shared[1], [128, NODES])
        dinv = carve(shared[1], [TB, NODES])
        for area in shared:
            area[1] = 0
        ones16 = sb("ones16", [EP, TB], BF16)
        ones = sb("ones", [TB, TB])
        reach = sb("reach", [EP, EC + 1])
        far_max = sb("far_max", [1, 1])
        far = sb("far", [1, 1], I32)
        degc = sb("degc", [TB, NB])
        dsrc = sb("dsrc", [TB, NB])
        xt = sb("xt", [KE, GRID, GRID * PATCH])
        X = over([TB, NB, 2 * D])
        H = over([128, NODES])
        hL = sb("hL", [TOK, NC, 2, D])
        hb = over([TOK, NC, 2, D])
        xc = over([TOK, 2 * NC, D])
        sq = over([TOK, 2 * NC, D])
        st = sb("st", [TOK, LAYERS, 5, 2 * NC])
        x1 = over([TOK, NC, 2, D])
        x1T = over([128, NC, TOK])
        kneg = sb("kneg", [128, 1])
        ksum = sb("ksum", [128, 1])
        kinv = sb("kinv", [128, 1])
        ET = over([128, NC, TOK])
        Ek = over([TOK, NC, 128])
        kx = over([128, 128])
        kq = over([128, 128])
        vkq = over([128, 128])
        zh = Ek.rearrange("p c f -> p (c f)").rearrange("p (h t e) -> p h t e", h=2 * HEADS, t=NC)
        zT = ET
        yn = over([TOK, NC, 2, D])
        x2s = over([TOK, NC, 2, 2, D], F16)
        lg = over([TOK, 2 * NC, EXPERTS])
        lg2 = over([TOK, 2 * NC, EXPERTS])
        hit = over([TOK, 2, 2 * NC, EXPERTS])
        ohot = over([TOK, 2, 2 * NC, EXPERTS])
        tv = sb("tv", [TOK, 10, 2 * NC])
        gT = over([128, 2, TOK])
        x2 = over([TOK, 2, NC, 2, D])
        hres = over([TOK, 2, NC, 2, D])
        x2T = sb("x2T", [128, 2, 2, SEQ], F16)
        gate = over([TOK, 2, 2 * NC, EXPERTS])
        base = over([TOK, 2, 2, NC, D])
        hid = over([FF, 4, GROUP])
        tmp = over([TOK, TMPS, 512])
        acc = over([TOK, 2, 4, 2, D])
        ys = over([TOK, NC, D])
        fxc = over([TOK, NC, D])
        fst = sb("fst", [TOK, 5, NC])
        fin = over([TOK, 2, NC, D])

        s_const = sem("const_loaded")
        s_wz = sem("weights_zeroed")
        s_wemb = sem("embedding_loaded")
        s_w = sem("weights_loaded")
        s_dst = sem("target_one_hots")
        s_edge = sem("edges_loaded")
        s_wx = sem("expert_weights_loaded")
        s_ef = sem("edges_float")
        s_hot = sem("one_hots")
        s_oned = sem("ones_set")
        s_turn = sem("weights_turned")
        s_wcopy = sem("turned_copied")
        s_inv = sem("powers_inverted")
        s_posb = sem("pos_biased")
        s_fold_ps = sem("embedding_folded_ps")
        s_fold = sem("embedding_folded")
        s_posx_ps = sem("pos_mixed_ps")
        s_posx = sem("pos_mixed")
        s_w1t = sem("w1_turned")
        s_w1c = sem("w1_scaled")
        s_w1hi = sem("w1_high_parts")
        s_w1p = sem("w1_split_turned")
        s_w1s = sem("w1_ready")
        s_gw = sem("gate_weights_split")
        s_cen = sem("output_weights_centred")
        s_degs = sem("degree_sums")
        s_deg = sem("degrees")
        s_diag = sem("degree_diagonals")
        s_dsrc = sem("source_roots")
        s_ddiag = sem("roots_on_diagonals")
        s_dinv_ps = sem("roots_spread")
        s_dinv = sem("target_roots")
        s_reach = sem("edge_reach")
        s_reachT = sem("edge_reach_turned")
        s_far = sem("far_edges_known")
        s_cnt = sem("edge_counts")
        s_adj = sem("adjacency")
        s_half = sem("exponent_set")
        counts = {
            "x_in": 192, "txt_in": 32, "embedded": 2, "mixed": 4, "nodes": 6,
            "aggregated": 6, "graph": 6, "tokens_ps": 2, "tokens": 3, "stat": 7, "centred": 2, "squared": 3,
            "variance": 3, "rstd": 3, "normed": 3, "x1_turned": 2, "x1T_ready": 2, "keys_ps": 1, "kmax": 1,
            "kexp": 1, "keys_turned": 2, "keys_ready": 2, "kx_ps": 1, "kx_ready": 1, "kq_ps": 1, "kq_ready": 2,
            "vkq_ps": 1, "vkq_ready": 1, "heads_ps": 2, "heads_a": 1, "heads_b": 1, "heads_turned": 2,
            "zT_ready": 2, "attn_ps": 2, "attn": 2, "gam": 1, "hbeta": 1, "hres": 1, "x2_parts": 2, "x2_turned": 2, "x2T_ready": 2,
            "logits_ps": 2, "top2": 16, "top2b": 1, "top2_exp": 1, "gates": 4, "gates_turned": 1, "gates_ready": 1, "bias2_ps": 2,
            "base": 2,
            "hidden_ps": STEPS, "hidden": STEPS, "outputs_ps": STEPS, "gated": UNITS, "added": UNITS - 4,
            "folded": 4, "summed": 4, "f_stat": 6, "f_centred": 2, "f_squared": 2, "f_variance": 2, "f_rstd": 2,
            "f_normed": 2, "f_gamma": 2, "f_beta": 1, "final": 2, "stored": 32,
        }
        sems = {k: sem("s_" + k) for k in counts}

        def after(eng, name, p, k):
            v = p * counts[name] + k
            if isinstance(v, int) and v <= 0:
                return
            eng.wait_ge(sems[name], v)

        def bc(ap, n):
            return ap.unsqueeze(2).to_broadcast([ap.shape[0], ap.shape[1], n])

        def rows(ap, g):
            return ap.unsqueeze(1).to_broadcast([ap.shape[0], g, ap.shape[1]])

        def flat(ap):
            return ap.rearrange("p c b d -> p (c b) d")

        def bank16(i):
            return F[:, i, :].bitcast(F16)

        block = ctx.enter_context(nc.Block())

        @block.sync
        def _(sp):
            def row_bc(dst, src, n):
                return sp.dma_start(dst[0:TOK, :], src.partition_broadcast(TOK))

            sp.dma_start(eidx[:], edges.rearrange("a (p j) -> p a j", j=EC)).then_inc(s_edge, 16)
            for d, s in ((iota, c_iota), (ident, c_ident)):
                sp.dma_start(d[:], s).then_inc(s_const, 16)

            def load_images(p):
                after(sp, "embedded", p, 0)
                for sh in range(2):
                    for b in range(2):
                        src = x[bass.ds(2 * p + b, 1)].rearrange("o c (i h) w -> (o c) h i w", h=PATCH)
                        w = GRID * PATCH - RUN * sh
                        for c in range(CH):
                            r = PATCH * (CH * (2 * sh + b) + c)
                            sp.dma_start(xt[r:r + PATCH, :, 0:w], src[c, :, :, RUN * sh:]
                                         ).then_inc(sems["x_in"], 16)

            sp.wait_ge(s_wz, 1)
            for b in range(2):
                r = slice(D * b, D * (b + 1))
                for sh in range(2):
                    q = CH * PATCH * (2 * sh + b)
                    sp.dma_start(wemb[q:q + CH * PATCH, :, r],
                                 W_embed.rearrange("(q w) d -> q w d", w=PATCH)[:, RUN * sh:RUN * (sh + 1), :]
                                 ).then_inc(s_wemb, 16)
                sp.dma_start(bemb[r, :], b_embed.rearrange("(d o) -> d o", o=1)).then_inc(s_wemb, 16)
                sp.dma_start(wg[r, :, r], W_gcn.rearrange("l k d -> k l d")).then_inc(s_wemb, 16)
            sp.dma_start(pos[:], c_pos).then_inc(s_wemb, 16)
            load_images(0)
            for b in range(2):
                r = slice(D * b, D * (b + 1))
                sp.dma_start(wtok[r, r], W_out).then_inc(s_w, 16)
                sp.dma_start(wq[r, r], Wqkv[:, 0:D]).then_inc(s_w, 16)
                sp.dma_start(wk[r, r], Wqkv[:, D:2 * D]).then_inc(s_w, 16)
                sp.dma_start(wv[r, r], Wqkv[:, 2 * D:3 * D]).then_inc(s_w, 16)
                sp.dma_start(watt[r, r], Wout).then_inc(s_w, 16)
                sp.dma_start(gw[r, :], gate_w).then_inc(s_w, 16)
                sp.dma_start(bg_rows[:, b, :], b_gcn).then_inc(s_w, 16)
            sp.dma_start(mask[:], c_mask).then_inc(s_w, 16)
            for d, s in ((btok, b_out), (batt, bout), (ga_b, ga), (ba_b, ba), (gf_b, gf), (bf_b, bf), (gateb, gate_b)):
                row_bc(d, s, s.shape[0]).then_inc(s_w, 16)
            sp.dma_start(w1n[:], w1.rearrange("e h f -> h e f")).then_inc(s_wx, 16)
            sp.dma_start(b1n[:], b1).then_inc(s_wx, 16)
            sp.dma_start(w2s[:], w2.rearrange("e f h -> f e h")).then_inc(s_wx, 16)
            for c in range(NC):
                sp.dma_start(b2d[EXPERTS * c:EXPERTS * (c + 1), c, :], b2).then_inc(s_wx, 16)

            def load_text(p):
                after(sp, "hbeta", p, 0)
                after(sp, "centred", p, 1 - 2)
                for b in range(2):
                    sp.dma_start(hL[LASTIMG:TOK, NC - 1, b, :], txt[bass.ds(2 * p + b, 1)].rearrange("o t d -> (o t) d")
                                 ).then_inc(sems["txt_in"], 16)

            def store(p, b):
                after(sp, "final", p, b + 1)
                sp.dma_start(out[bass.ds(2 * p + b, 1)].rearrange("o (c t) d -> (o t) c d", t=TOK), fin[:, b]
                             ).then_inc(sems["stored"], 16)

            load_text(0)
            load_images(1)
            for p in (1, 2):
                load_text(p)
                load_images(p + 1)
            store(0, 0)
            with sp.Fori(3, PAIRS - 1) as p:
                load_text(p)
                load_images(p + 1)
                store(p - 3, 1)
                store(p - 2, 0)
            load_text(PAIRS - 1)
            for p in range(PAIRS - 4, PAIRS):
                if p > PAIRS - 4:
                    store(p, 0)
                store(p, 1)
            sp.wait_ge(sems["stored"], 32 * PAIRS)

        def run(eng, name, front_step, ffn_step, final_step, setup_step=None):

            def put(steps, step, n, p, par):
                for what, where, idx, slot in steps:
                    if where == name and slot == n:
                        step(what, idx, p, par)

            def body(ahead, front, par, ffn, fpar, tail, setup=None):
                for n in range(STEPS):
                    if ffn is not None:
                        ffn_step(ffn, fpar, n)
                    if tail:
                        put(FINAL_1, final_step, n, ffn - 1, 1 - fpar)
                    if ffn is not None:
                        put(FINAL_0, final_step, n, ffn, fpar)
                    if front is not None:
                        put(ATTENTION, front_step, n, front, par)
                    if ahead is not None:
                        put(GRAPH[2:] if setup == 0 else GRAPH, front_step, n, ahead, par)
                    if setup is not None:
                        put(WEIGHTS[setup], setup_step, n, 0, 0)

            body(0, None, None, None, None, False, setup=0)
            body(1, 0, 0, None, None, False, setup=1)
            body(2, 1, 1, 0, 0, False)
            body(3, 2, 0, 1, 1, True)
            with eng.Fori(0, (PAIRS - 4) // 2) as i:
                body(2 * i + 4, 2 * i + 3, 1, 2 * i + 2, 0, True)
                body(2 * i + 5, 2 * i + 4, 0, 2 * i + 3, 1, True)
            body(None, PAIRS - 1, 1, PAIRS - 2, 0, True)
            body(None, None, None, PAIRS - 1, 1, True)
            for n in range(STEPS):
                put(FINAL_1, final_step, n, PAIRS - 1, 1)

        NW = 2 * 7 + 8

        @block.tensor
        def _(pe):
            mm, tr = pe.matmul, pe.transpose

            def embed(p, idx):
                if idx == 0:
                    after(pe, "x_in", p, 192)
                    after(pe, "tokens", p, 0)
                px = xt[:].rearrange("p i (j w) -> p (i j) w", w=PATCH)
                for t in range(4 * idx, min(4 * idx + 4, NB)):
                    for w in range(RUN):
                        m = mm(F[0:TB, idx, 128 * (t % 4):128 * (t % 4 + 1)], px[:, TB * t:TB * (t + 1), w],
                               wemb[:, w, :], start=(w == 0), stop=(w == RUN - 1))
                m.then_inc(sems["embedded"], 1)

            pe.wait_ge(s_oned, 2)
            for j in range(EC):
                pe.wait_ge(s_dst, j + 1)
                mm(O[0:TB, 0, 0:4 * TB], ones16[:], hot[:, 1, j, 0:4 * TB], start=(j == 0), stop=(j == EC - 1))
                m = mm(O[0:TB, 1, 0:3 * TB], ones16[:], hot[:, 1, j, 4 * TB:], start=(j == 0), stop=(j == EC - 1))
            m.then_inc(s_degs, 1)
            pe.wait_ge(s_reach, 2)
            tr(F[0:1, 2, 0:EP], reach[:, EC:EC + 1], ident[0:EP, 0:EP]).then_inc(s_reachT, 1)
            pe.wait_ge(s_wemb, 16 * 9)
            for w in range(RUN):
                t = tr(F[:, 0, KE * w:KE * (w + 1)], wemb[:, w, :], ident[0:KE, 0:KE])
            t.then_inc(s_fold_ps, 1)
            pe.wait_ge(s_posb, 1)
            for t in range(NB):
                m = mm(Z[0:TB, t // 4, 128 * (t % 4):128 * (t % 4 + 1)], pos[:, TB * t:TB * (t + 1)], wg[:, 0, :],
                       start=True, stop=True)
            m.then_inc(s_posx_ps, 1)
            pe.wait_ge(s_fold, 1)
            for w in range(RUN):
                m = mm(F[0:KE, 1, 128 * w:128 * (w + 1)], wembT[:, w, :], wg[:, 0, :], start=True, stop=True)
            m.then_inc(s_fold_ps, 1)
            pe.wait_ge(s_fold, 2)
            embed(0, 0)
            embed(0, 1)
            pe.wait_ge(s_ddiag, 1)
            pe.wait_ge(s_far, 1)
            for h, k in ((0, 4), (1, 3)):
                m = mm(F[0:TB, 2 + h, 0:TB * k], ones[:], ddiag[:, 4 * h:4 * h + k, :].rearrange("p t m -> p (t m)"),
                       start=True, stop=True)
            m.then_inc(s_dinv_ps, 1)
            far_pe = pe.value_load(far[0:1, 0:1], min_val=0, max_val=1)
            pe.wait_ge(s_posx, 2)
            pe.wait_ge(s_hot, 1)

            def count(q, t, n0, n1, inc):
                if q >= 4:
                    pe.wait_ge(s_adj, inc * (q - 3))
                bank = (Z if q % 4 < 2 else O)[0:TB, q % 2, :]
                s0, s1 = max(n0, TB * t), min(n1, TB * (t + 1))
                for j in range(EC):
                    m = mm(bank[:, 0:n1 - n0], hot[:, 0, j, TB * t:TB * (t + 1)], hot[:, 1, j, n0:n1],
                           start=(j == 0), stop=(j == EC - 1), skip_group_check=True)
                    if j == 0 and s0 < s1:
                        mm(bank[:, s0 - n0:s1 - n0], identb[:], identb[:, s0 - TB * t:s1 - TB * t],
                           start=False, stop=False, skip_group_check=True)
                m.then_inc(s_cnt, inc)

            with pe.If(far_pe):
                for q in range(2 * NB):
                    count(q, q // 2, HALF * (q % 2), HALF * (q % 2 + 1), 1)
            with pe.Else():
                for t in range(NB):
                    count(t, t, *window(t), 2)
            pe.wait_ge(s_dinv, 2)
            pe.wait_ge(s_w, 16 * NW)
            pe.wait_ge(s_wx, 16 * (3 + NC))
            tr(F[:, 3, 0:LAYERS], bg_rows[:].rearrange("l b d -> l (b d)"), ident[0:LAYERS, 0:LAYERS])
            tr(F[:, 3, 192:320], wv[:], ident[:])
            tr(F[:, 3, 320:336], b1n[:], ident[0:EXPERTS, 0:EXPERTS]).then_inc(s_turn, 1)

            def setup_step(what, idx, p, par):
                if what == "w1_turn":
                    pe.wait_ge(s_adj, 2 * NB)
                    for e in range(EXPERTS):
                        t = tr(Z[:, e // 8, D * (e % 8):D * (e % 8 + 1)], w1n[:, e, :], ident[0:D, 0:D])
                    t.then_inc(s_w1t, 1)
                elif what == "w1_back":
                    pe.wait_ge(s_w1c, 6)
                    for e in range(EXPERTS):
                        dst = (O if idx == 0 else Z)[:, e // 8, :].bitcast(F16)
                        t = tr(dst[:, FF * (e % 8):FF * (e % 8 + 1)], w1T[:, idx, e].rearrange("f u k -> f (u k)"),
                               ident16[:])
                    t.then_inc(s_w1p, 1)

            def front_step(what, idx, p, par):
                if what == "embed":
                    embed(p, idx)
                elif what == "node_mix":
                    after(pe, "graph", p, 2 * idx)
                    for t in range(NB):
                        m = mm(F[0:TB, t // 4, 128 * (t % 4):128 * (t % 4 + 1)], H[:, TB * t:TB * (t + 1)],
                               wg[:, idx, :], start=True, stop=True)
                        if t in (3, 6):
                            m.then_inc(sems["mixed"], 1)
                elif what == "aggregate":
                    after(pe, "nodes", p, 2 * idx + 2)
                    with pe.If(far_pe):
                        for h in range(2):
                            for t in range(NB):
                                m = mm(F[:, h, 0:HALF], X[:, t, :], adj[:, t, HALF * h:HALF * (h + 1)],
                                       start=(t == 0), stop=(t == NB - 1))
                            m.then_inc(sems["aggregated"], 1)
                    with pe.Else():
                        for h in range(2):
                            near = [t for t in range(NB) if window(t)[0] < HALF * (h + 1) and window(t)[1] > HALF * h]
                            for t in near:
                                n0, n1 = max(window(t)[0], HALF * h), min(window(t)[1], HALF * (h + 1))
                                m = mm(F[:, h, n0 - HALF * h:n1 - HALF * h], X[:, t, :], adj[:, t, n0:n1],
                                       start=(t == near[0]), stop=(t == near[-1]), skip_group_check=True)
                            m.then_inc(sems["aggregated"], 1)
                elif what == "tokens":
                    after(pe, "graph", p, 6)
                    for c in range(NC):
                        n = TOK if c < NC - 1 else LASTIMG
                        m = mm(F[0:n, c // 4, 128 * (c % 4):128 * (c % 4 + 1)], H[:, TOK * c:TOK * c + n], wtok[:],
                               start=True, stop=True)
                        if c % 4 == 3:
                            m.then_inc(sems["tokens_ps"], 1)
                elif what == "x1_turn":
                    after(pe, "normed", p, 1)
                    for c in range(NC):
                        t = tr(F[:, 2 + c // 4, TOK * (c % 4):TOK * (c % 4 + 1)],
                               x1[:, c].rearrange("p b d -> p (b d)"), ident[0:TOK, 0:TOK])
                        if c % 4 == 3:
                            t.then_inc(sems["x1_turned"], 1)
                elif what == "keys":
                    after(pe, "x1T_ready", p, 2)
                    for h in range(2):
                        m = mm(F[:, 2 + h, 0:GROUP], wk[:], x1T[:, 4 * h:4 * h + 4, :].rearrange("p c t -> p (c t)"),
                               start=True, stop=True)
                    m.then_inc(sems["keys_ps"], 1)
                elif what == "keys_turn":
                    after(pe, "kexp", p, 1)
                    for c in range(NC):
                        t = tr(F[0:TOK, 2 + c // 4, 128 * (c % 4):128 * (c % 4 + 1)], ET[:, c, :], ident[:])
                        if c % 4 == 3:
                            t.then_inc(sems["keys_turned"], 1)
                elif what == "kx":
                    after(pe, "keys_ready", p, 2)
                    for c in range(NC):
                        m = mm(F[:, 2, 0:128], x1[:, c].rearrange("p b d -> p (b d)"), Ek[:, c, :],
                               start=(c == 0), stop=(c == NC - 1))
                    m.then_inc(sems["kx_ps"], 1)
                elif what == "kq":
                    after(pe, "kx_ready", p, 1)
                    mm(F[:, 3, 0:128], kx[:], wq[:], start=True, stop=True).then_inc(sems["kq_ps"], 1)
                elif what == "vkq":
                    after(pe, "kq_ready", p, 2)
                    mm(F[:, 2, 0:128], wvT[:], kq[:], start=True, stop=True).then_inc(sems["vkq_ps"], 1)
                elif what == "heads":
                    after(pe, "vkq_ready", p, 1)
                    xs = x1T[:].rearrange("p c t -> p (c t)").rearrange("p (m t) -> p t m", t=NC)
                    for t in range(NC):
                        m = mm(F[0:TOK, 2 + t // 4, 128 * (t % 4):128 * (t % 4 + 1)], xs[:, t, :], vkq[:],
                               start=True, stop=True)
                        if t % 4 == 3:
                            m.then_inc(sems["heads_ps"], 1)
                elif what == "heads_turn":
                    after(pe, "heads_a", p, 1)
                    after(pe, "heads_b", p, 1)
                    for hp in range(HEADS):
                        t = tr(F[:, 2 + hp // 4, TOK * (hp % 4):TOK * (hp % 4 + 1)],
                               zh[:, 2 * hp:2 * hp + 2].rearrange("p h t e -> p (h t e)"), ident[0:TOK, 0:TOK])
                        if hp % 4 == 3:
                            t.then_inc(sems["heads_turned"], 1)
                elif what == "attn_out":
                    after(pe, "zT_ready", p, 2)
                    if isinstance(p, int) and p == 0:
                        pe.wait_ge(s_cen, 6)
                    for hp in range(HEADS):
                        m = mm(F[0:TOK, 2 + hp // 4, 128 * (hp % 4):128 * (hp % 4 + 1)], zT[:, hp, :], watt[:],
                               start=True, stop=True)
                        if hp % 4 == 3:
                            m.then_inc(sems["attn_ps"], 1)
                elif what == "x2_turn":
                    after(pe, "x2_parts", p, 2)
                    for b in range(2):
                        for c in range(NC):
                            t = tr(bank16(2 + b)[:, TOK * c:TOK * (c + 1)], x2s[:, c, b].rearrange("p u d -> p (u d)"),
                                   ident16[0:TOK, 0:TOK])
                        t.then_inc(sems["x2_turned"], 1)
                elif what == "logits":
                    after(pe, "x2T_ready", p, 2)
                    if isinstance(p, int) and p == 0:
                        pe.wait_ge(s_gw, 5)
                    for b in range(2):
                        for c in range(NC):
                            m = mm(F[0:TOK, 2 + b, 48 * c:48 * (c + 1)], x2T[:, par, b, TOK * c:TOK * (c + 1)],
                                   gw3[:].rearrange("p u e -> p (u e)"), start=True, stop=True)
                        m.then_inc(sems["logits_ps"], 1)
                elif what == "gates_turn":
                    after(pe, "gates", p, 4)
                    for b in range(2):
                        t = tr(F[:, 2, TOK * b:TOK * (b + 1)],
                               gate[:, par, NC * b:NC * (b + 1), :].rearrange("p c e -> p (c e)"), ident[0:TOK, 0:TOK])
                    t.then_inc(sems["gates_turned"], 1)
                elif what == "bias2":
                    after(pe, "gates_ready", p, 1)
                    for b in range(2):
                        mm(F[0:TOK, 2 + b, :], gT[:, b, :], b2d[:].rearrange("p c d -> p (c d)"),
                           start=True, stop=True).then_inc(sems["bias2_ps"], 1)

            def hidden(p, par, n):
                g, e = divmod(n, EXPERTS)
                if n == 0:
                    after(pe, "x2T_ready", p, 2)
                    if isinstance(p, int) and p == 0:
                        pe.wait_ge(s_w1s, 2)
                after(pe, "hidden", p, n - 1)
                for part in range(2):
                    m = mm(Z[:, n % 2, 0:GROUP], w1s[:, part, e, :],
                           x2T[:, par, g // 2, GROUP * (g % 2):GROUP * (g % 2 + 1)],
                           start=(part == 0), stop=(part == 1))
                m.then_inc(sems["hidden_ps"], 1)

            def ffn_step(p, par, n):
                if n == 0:
                    hidden(p, par, 0)
                    hidden(p, par, 1)
                if n + 2 < STEPS:
                    hidden(p, par, n + 2)
                u = n // 2
                if n % 2 == 0:
                    after(pe, "gated", p, u - 1)
                after(pe, "hidden", p, n + 1)
                for c in range(4):
                    m = mm(O[0:TOK, u % 2, 128 * c + D * (n % 2):128 * c + D * (n % 2 + 1)],
                           hid[:, n % 4, TOK * c:TOK * (c + 1)], w2s[:, n % EXPERTS, :], start=True, stop=True)
                m.then_inc(sems["outputs_ps"], 1)

            run(pe, "pe", front_step, ffn_step, None, setup_step)

        @block.scalar
        def _(act):
            act.wait_ge(s_wemb, 16 * 9)
            act.activation(pos, pos, ACT.Identity, bias=bemb[:]).then_inc(s_posb, 1)
            act.wait_ge(s_fold_ps, 1)
            act.copy(wembT.rearrange("p w k -> p (w k)"), F[:, 0, 0:KE * RUN]).then_inc(s_fold, 1)
            act.wait_ge(s_fold_ps, 2)
            act.copy(wemb[:].rearrange("p w d -> p (w d)"), F[0:KE, 1, :]).then_inc(s_fold, 1)
            act.wait_ge(s_posx_ps, 1)
            for h, k in ((0, 4), (1, 3)):
                act.copy(posx[:, 4 * h:4 * h + k, :].rearrange("p t d -> p (t d)"), Z[0:TB, h, 0:128 * k]
                         ).then_inc(s_posx, 1)
            act.wait_ge(s_dinv_ps, 1)
            act.copy(dinv[:, 0:4 * TB], F[0:TB, 2, 0:4 * TB]).then_inc(s_dinv, 1)
            act.copy(dinv[:, 4 * TB:], F[0:TB, 3, 0:3 * TB]).then_inc(s_dinv, 1)
            act.wait_ge(s_wcopy, 2)

            def setup_step(what, idx, p, par):
                if what == "w1_out":
                    act.wait_ge(s_w1p, idx + 1)
                    act.copy(w1s[:, idx].rearrange("p (h e) f -> p h (e f)", h=2), (Z if idx else O)[:].bitcast(F16)
                             ).then_inc(s_w1s, 1)

            def front_step(what, idx, p, par):
                if what == "graph_relu":
                    for h in range(2):
                        after(act, "aggregated", p, 2 * idx + h + 1)
                        act.activation(H[:, HALF * h:HALF * (h + 1)], F[:, h, 0:HALF], ACT.Relu,
                                       bias=bg[:, idx:idx + 1]).then_inc(sems["graph"], 1)
                elif what == "ln_square":
                    after(act, *(("centred", p, 1), ("attn", p, 2), ("centred", p, 2))[idx])
                    act.activation(sq[:], xc[:], ACT.Square).then_inc(sems["squared"], 1)
                elif what == "x1_copy":
                    for h in range(2):
                        after(act, "x1_turned", p, h + 1)
                        act.copy(x1T[:, 4 * h:4 * h + 4, :].rearrange("p c t -> p (c t)"), F[:, 2 + h, 0:GROUP]
                                 ).then_inc(sems["x1T_ready"], 1)
                elif what == "keys_exp":
                    after(act, "kmax", p, 1)
                    act.activation(ET[:].rearrange("p (h c) t -> p h (c t)", h=2), F[:, 2:4, 0:GROUP], ACT.Exp,
                                   bias=kneg[:], accum_out=ksum[:]).then_inc(sems["kexp"], 1)
                elif what == "heads_copy":
                    after(act, "heads_ps", p, 2)
                    act.copy(zh[:, :, 4:8, :].rearrange("p h t e -> p t h e"),
                             F[0:TOK, 3, :].rearrange("p (t h e) -> p t h e", t=4, e=DH)).then_inc(sems["heads_b"], 1)
                elif what == "heads_turned":
                    for h in range(2):
                        after(act, "heads_turned", p, h + 1)
                        act.copy(zT[:, 4 * h:4 * h + 4, :].rearrange("p c t -> p (c t)"), F[:, 2 + h, 0:GROUP]
                                 ).then_inc(sems["zT_ready"], 1)
                elif what == "x2_copy":
                    for b in range(2):
                        after(act, "x2_turned", p, b + 1)
                        act.copy(x2T[:, par, b, :], bank16(2 + b)[:, 0:SEQ]).then_inc(sems["x2T_ready"], 1)
                elif what == "top2_exp":
                    after(act, "top2", p, 10)
                    act.activation(tv[:, 5], tv[:, 4], ACT.Exp).then_inc(sems["top2_exp"], 1)

            def ffn_step(p, par, n):
                if isinstance(p, int) and p == 0 and n == 0:
                    act.wait_ge(s_wcopy, 4)
                after(act, "hidden_ps", p, n + 1)
                after(act, "outputs_ps", p, n - 3)
                act.activation(hid[:, n % 4, :], Z[:, n % 2, 0:GROUP], ACT.Relu,
                               bias=b1s[:, n % EXPERTS:n % EXPERTS + 1]).then_inc(sems["hidden"], 1)

            def final_step(what, b, p, par):
                if what == "f_square":
                    after(act, "f_centred", p, b + 1)
                    after(act, "stored", p, 0)
                    act.activation(fin[:, b], fxc[:], ACT.Square).then_inc(sems["f_squared"], 1)

            run(act, "act", front_step, ffn_step, final_step, setup_step)

        @block.vector
        def _(dve):
            tt, ts, cp = dve.tensor_tensor, dve.tensor_scalar, dve.tensor_copy
            dve.wait_ge(s_edge, 16)
            cp(ef[:], eidx[:]).then_inc(s_ef, 1)
            dve.wait_ge(s_const, 32)
            cp(iota16[:], iota).then_inc(s_ef, 1)
            cp(identb[:], ident[0:TB, 0:TB]).then_inc(s_ef, 1)
            cp(ident16[:], ident[:]).then_inc(s_ef, 1)
            dve.wait_ge(s_ef, 4)

            def one_hots(a, j0, j1):
                for j in range(j0, j1):
                    m = ts(hot[:, a, j, :], iota16[0:EP, :], ef[:, a, j:j + 1], None, ALU.is_equal)
                    if a == 1:
                        m.then_inc(s_dst, 1)
                return m

            one_hots(1, 0, EC)
            tt(reach[:, 0:EC], ef[:, 0, :], ef[:, 1, :], ALU.subtract).then_inc(s_reach, 1)
            dve.wait_ge(s_reach, 1)
            dve.tensor_reduce(reach[:, EC:EC + 1], reach[:, 0:EC], AX.X, ALU.max, apply_absolute_value=True
                              ).then_inc(s_reach, 1)
            one_hots(0, 0, 3)
            dve.wait_ge(s_degs, 1)
            for h, k in ((0, 4), (1, 3)):
                tt(ddiag[:, 4 * h:4 * h + k, :], O[0:TB, h, 0:TB * k].rearrange("p (t m) -> p t m", m=TB),
                   rows(ident[0:TB, 0:TB], k), ALU.mult).then_inc(s_diag, 1)
            dve.wait_ge(s_diag, 2)
            dve.tensor_reduce(degc[:], ddiag, AX.X, ALU.add).then_inc(s_diag, 1)
            dve.wait_ge(s_diag, 3)
            ts(degc[:], degc[:], 1.0, None, ALU.add).then_inc(s_deg, 1)
            one_hots(0, 3, 12)
            dve.wait_ge(s_reachT, 1)
            dve.tensor_reduce(far_max[:], F[0:1, 2, 0:EP], AX.X, ALU.max).then_inc(s_reach, 1)
            dve.wait_ge(s_reach, 3)
            ts(far[:], far_max[:], float(REACH), None, ALU.is_gt).then_inc(s_far, 1)
            dve.wait_ge(s_dsrc, 1)
            tt(ddiag, rows(ident[0:TB, 0:TB], NB), bc(dsrc[:], TB), ALU.mult).then_inc(s_ddiag, 1)
            one_hots(0, 12, EC).then_inc(s_hot, 1)
            dve.wait_ge(s_far, 1)
            far_dve = dve.value_load(far[0:1, 0:1], min_val=0, max_val=1)
            dve.wait_ge(s_dinv, 2)

            def weigh(q, t, n0, n1, inc):
                dve.wait_ge(s_cnt, inc * (q + 1))
                dve.scalar_tensor_tensor(adj[:, t, n0:n1], (Z if q % 4 < 2 else O)[0:TB, q % 2, 0:n1 - n0],
                                         dsrc[:, t:t + 1], dinv[:, n0:n1], ALU.mult, ALU.mult).then_inc(s_adj, inc)

            with dve.If(far_dve):
                for q in range(2 * NB):
                    weigh(q, q // 2, HALF * (q % 2), HALF * (q % 2 + 1), 1)
            with dve.Else():
                for t in range(NB):
                    weigh(t, t, *window(t), 2)
            dve.wait_ge(s_turn, 1)
            cp(bg[:], F[:, 3, 0:LAYERS]).then_inc(s_wcopy, 1)
            cp(wvT[:], F[:, 3, 192:320]).then_inc(s_wcopy, 1)
            cp(b1s[:], F[:, 3, 320:336]).then_inc(s_wcopy, 1)

            def setup_step(what, idx, p, par):
                if what == "w1_max":
                    dve.wait_ge(s_w1t, 1)
                    for h in range(2):
                        dve.tensor_reduce(w1max[:, 8 * h:8 * h + 8], Z[:, h, :].rearrange("p (e k) -> p e k", k=D),
                                          AX.X, ALU.max, apply_absolute_value=True).then_inc(s_w1c, 1)
                    dve.wait_ge(s_w1c, 2)
                    ts(w1max[:], w1max[:], TINY, None, ALU.max).then_inc(s_w1c, 1)
                    dve.wait_ge(s_w1c, 3)
                    ts(w1pow[:].bitcast(I32), w1max[:].bitcast(I32), 0x7F800000, None, ALU.bitwise_and
                       ).then_inc(s_w1c, 1)
                    dve.wait_ge(s_w1c, 4)
                    dve.reciprocal(w1inv[:], w1pow[:]).then_inc(s_inv, 1)
                elif what == "w1_scale":
                    dve.wait_ge(s_inv, 1)
                    dve.wait_ge(s_wcopy, 3)
                    tt(b1s[:], b1s[:], w1inv[:], ALU.mult).then_inc(s_wcopy, 1)
                    for h in range(2):
                        m = tt(w1sc[:, 8 * h:8 * h + 8, :], Z[:, h, :].rearrange("p (e k) -> p e k", k=D),
                               bc(w1inv[:, 8 * h:8 * h + 8], D), ALU.mult)
                    m.then_inc(s_w1c, 1)
                elif what == "w2_scale":
                    tt(w2s[:], w2s[:], bc(w1pow[:], D), ALU.mult)
                elif what == "w1_hi":
                    dve.wait_ge(s_w1c, 5)
                    for u in range(2):
                        m = cp(w1T[:, 0, :, u, :], w1sc[:])
                    m.then_inc(s_w1hi, 1)
                elif what == "w1_lo":
                    dve.wait_ge(s_w1hi, 1)
                    m = tt(w1T[:, 1, :, idx, :], w1sc[:], w1T[:, 0, :, idx, :], ALU.subtract)
                    if idx == 1:
                        m.then_inc(s_w1c, 1)
                elif what == "gate_parts":
                    cp(gw3[:, 0, :], gw[:]).then_inc(s_gw, 1)
                    dve.wait_ge(s_gw, 1)
                    tt(gwr[:, 0, :], gw[:], gw3[:, 0, :], ALU.subtract).then_inc(s_gw, 1)
                    dve.wait_ge(s_gw, 2)
                    cp(gw3[:, 1, :], gwr[:, 0, :]).then_inc(s_gw, 1)
                    dve.wait_ge(s_gw, 3)
                    tt(gwr[:, 1, :], gwr[:, 0, :], gw3[:, 1, :], ALU.subtract).then_inc(s_gw, 1)
                    dve.wait_ge(s_gw, 4)
                    cp(gw3[:, 2, :], gwr[:, 1, :]).then_inc(s_gw, 1)
                elif what == "centre":
                    dve.tensor_reduce(wmean[:, 0:2], watt[:].rearrange("p (b d) -> p b d", b=2), AX.X, ALU.add
                                      ).then_inc(s_cen, 1)
                    dve.tensor_reduce(wmean[0:TOK, 2:3], batt[:], AX.X, ALU.add).then_inc(s_cen, 1)
                    dve.wait_ge(s_cen, 2)
                    ts(wmean[:, 0:2], wmean[:, 0:2], -1.0 / D, None, ALU.mult).then_inc(s_cen, 1)
                    ts(wmean[0:TOK, 2:3], wmean[0:TOK, 2:3], -1.0 / D, None, ALU.mult).then_inc(s_cen, 1)
                    dve.wait_ge(s_cen, 4)
                    tt(watt[:].rearrange("p (b d) -> p b d", b=2), watt[:].rearrange("p (b d) -> p b d", b=2),
                       bc(wmean[:, 0:2], D), ALU.add).then_inc(s_cen, 1)
                    ts(batt[:], batt[:], wmean[0:TOK, 2:3], None, ALU.add).then_inc(s_cen, 1)

            STAT0 = (0, 1, 4)

            def ln_sum(src, stats, groups, pre):
                dve.tensor_reduce(stats[:, 0, 0:groups], src, AX.X, ALU.add).then_inc(sems[pre + "stat"], 1)

            def ln_sub(src, dst_c, stats, groups, p, n0, pre):
                after(dve, pre + "stat", p, n0 + 1)
                ts(stats[:, 1, 0:groups], stats[:, 0, 0:groups], -1.0 / D, None, ALU.mult
                   ).then_inc(sems[pre + "stat"], 1)
                after(dve, pre + "stat", p, n0 + 2)
                tt(dst_c, src, bc(stats[:, 1, 0:groups], D), ALU.add).then_inc(sems[pre + "centred"], 1)

            def ln_var(sqv, stats, groups, p, k, n0, pre):
                after(dve, pre + "squared", p, k + 1)
                dve.tensor_reduce(stats[:, 2, 0:groups], sqv, AX.X, ALU.add).then_inc(sems[pre + "stat"], 1)
                after(dve, pre + "stat", p, n0 + 3)
                ts(stats[:, 3, 0:groups], stats[:, 2, 0:groups], 1.0 / D, EPS, ALU.mult, ALU.add
                   ).then_inc(sems[pre + "variance"], 1)

            def front_step(what, idx, p, par):
                if what == "node_copy":
                    for h, (t0, t1) in enumerate(((0, 4), (4, 7))):
                        ps = F[0:TB, h, 0:128 * (t1 - t0)]
                        dst = X[:, t0:t1, :].rearrange("p t f -> p (t f)")
                        if idx == 0:
                            after(dve, "embedded", p, h + 1)
                            after(dve, "aggregated", p, 0)
                            if isinstance(p, int) and p == 0:
                                dve.wait_ge(s_posx, 2)
                            tt(dst, ps, posx[:, t0:t1, :].rearrange("p t f -> p (t f)"), ALU.add
                               ).then_inc(sems["nodes"], 1)
                        else:
                            after(dve, "mixed", p, 2 * idx + h - 1)
                            after(dve, "aggregated", p, 2 * idx)
                            cp(dst, ps).then_inc(sems["nodes"], 1)
                elif what == "tokens_copy":
                    after(dve, "tokens_ps", p, 2)
                    after(dve, "hbeta", p, 0)
                    after(dve, "centred", p, 1 - 2)
                    after(dve, "txt_in", p, 32)
                    bt = rows(btok[:], 8)
                    tt(flat(hL[:, 0:4]), F[0:TOK, 0, :].rearrange("p (c d) -> p c d", d=D), bt, ALU.add
                       ).then_inc(sems["tokens"], 1)
                    tt(flat(hL[:, 4:7]), F[0:TOK, 1, 0:384].rearrange("p (c d) -> p c d", d=D), bt[:, 0:6], ALU.add
                       ).then_inc(sems["tokens"], 1)
                    tt(hL[0:LASTIMG, 7], F[0:LASTIMG, 1, 384:512].rearrange("p (c d) -> p c d", d=D),
                       bt[0:LASTIMG, 0:2], ALU.add).then_inc(sems["tokens"], 1)
                elif what in ("ln_sum", "ln_sub"):
                    src = (flat(hL[:]), None, flat(hres[:, par]))[idx]
                    if what == "ln_sum":
                        after(dve, *(("tokens", p, 3), None, ("hres", p, 1))[idx])
                        ln_sum(src, st[:, idx], 2 * NC, "")
                    else:
                        ln_sub(src, xc[:], st[:, idx], 2 * NC, p, STAT0[idx], "")
                elif what == "ln_var":
                    ln_var(sq[:], st[:, idx], 2 * NC, p, idx, STAT0[idx], "")
                elif what == "ln_apply":
                    after(dve, "rstd", p, idx + 1)
                    if idx == 2:
                        after(dve, "summed", p - 2, 4)
                    if idx == 1:
                        after(dve, "gam", p, 1)
                    src = flat(yn[:]) if idx == 1 else xc[:]
                    dst = (flat(x1[:]), flat(yn[:]), flat(x2[:, par]))[idx]
                    tt(dst, src, bc(st[:, idx, 4], D), ALU.mult).then_inc(sems["normed"], 1)
                elif what == "keys_max":
                    after(dve, "keys_ps", p, 1)
                    dve.tensor_reduce(kneg[:], F[:, 2:4, 0:GROUP], AX.XY, ALU.max, negate=True
                                      ).then_inc(sems["kmax"], 1)
                elif what == "keys_copy":
                    for h in range(2):
                        after(dve, "keys_turned", p, h + 1)
                        cp(Ek[:, 4 * h:4 * h + 4, :].rearrange("p c f -> p (c f)"), F[0:TOK, 2 + h, :]
                           ).then_inc(sems["keys_ready"], 1)
                elif what == "kx_copy":
                    after(dve, "kx_ps", p, 1)
                    cp(kx[:], F[:, 2, 0:128]).then_inc(sems["kx_ready"], 1)
                elif what == "kq_mask":
                    dve.reciprocal(kinv[:], ksum[:]).then_inc(sems["kq_ready"], 1)
                    after(dve, "kq_ready", p, 1)
                    after(dve, "kq_ps", p, 1)
                    dve.scalar_tensor_tensor(kq[:], F[:, 3, 0:128], kinv[:], mask[:], ALU.mult, ALU.mult
                                             ).then_inc(sems["kq_ready"], 1)
                elif what == "vkq_copy":
                    after(dve, "vkq_ps", p, 1)
                    cp(vkq[:], F[:, 2, 0:128]).then_inc(sems["vkq_ready"], 1)
                elif what == "heads_copy":
                    after(dve, "heads_ps", p, 1)
                    cp(zh[:, :, 0:4, :].rearrange("p h t e -> p t h e"),
                       F[0:TOK, 2, :].rearrange("p (t h e) -> p t h e", t=4, e=DH)).then_inc(sems["heads_a"], 1)
                elif what == "attn_bias":
                    if isinstance(p, int) and p == 0:
                        dve.wait_ge(s_cen, 6)
                    for b in range(2):
                        after(dve, "attn_ps", p, b + 1)
                        tt(xc[:].rearrange("p (c b) d -> p c b d", b=2)[:, :, b, :], F[0:TOK, 2 + b, :].rearrange("p (c d) -> p c d", d=D), rows(batt[:], NC),
                           ALU.add).then_inc(sems["attn"], 1)
                elif what == "res_gamma":
                    after(dve, "attn", p, 2)
                    tt(flat(yn[:]), xc[:], rows(ga_b[:], 2 * NC), ALU.mult).then_inc(sems["gam"], 1)
                elif what == "res_beta":
                    after(dve, "normed", p, 2)
                    after(dve, "hbeta", p, 1)
                    after(dve, "final", p - 2, 2)
                    tt(flat(hres[:, par]), flat(yn[:]), flat(hb[:]), ALU.add).then_inc(sems["hres"], 1)
                elif what == "x2_hi":
                    after(dve, "normed", p, 3)
                    cp(x2s[:, :, :, 0, :], x2[:, par]).then_inc(sems["x2_parts"], 1)
                elif what == "x2_lo":
                    v = x2[:, par]
                    after(dve, "x2_parts", p, 1)
                    tt(x2s[:, :, :, 1, :], v, x2s[:, :, :, 0, :], ALU.subtract).then_inc(sems["x2_parts"], 1)
                elif what == "top2_sum":
                    for b in range(2):
                        after(dve, "logits_ps", p, b + 1)
                        dve.tensor_reduce(lg[:, NC * b:NC * (b + 1), :],
                                          F[0:TOK, 2 + b, 0:48 * NC].rearrange("p (c u e) -> p c e u", u=3, e=EXPERTS),
                                          AX.X, ALU.add).then_inc(sems["top2"], 1)
                    after(dve, "top2", p, 2)
                    tt(lg[:], lg[:], rows(gateb[:], 2 * NC), ALU.add).then_inc(sems["top2"], 1)
                elif what == "top2_a":
                    after(dve, "top2", p, 3)
                    top(lg, 0, p, 3)
                elif what == "top2_b":
                    dve.scalar_tensor_tensor(lg2[:], ohot[:, 0], -HUGE, lg[:], ALU.mult, ALU.add
                                             ).then_inc(sems["top2"], 1)
                    after(dve, "top2", p, 8)
                    dve.tensor_reduce(tv[:, 1], lg2[:], AX.X, ALU.max).then_inc(sems["top2"], 1)
                    after(dve, "top2", p, 9)
                    tt(tv[:, 4], tv[:, 1], tv[:, 0], ALU.subtract).then_inc(sems["top2"], 1)
                elif what == "top2_c":
                    tt(hit[:, 1], lg2[:], bc(tv[:, 1], EXPERTS), ALU.is_equal).then_inc(sems["top2"], 1)
                    after(dve, "top2", p, 11)
                    tt(hit[:, 1], hit[:, 1], rows(rev[:], 2 * NC), ALU.mult).then_inc(sems["top2"], 1)
                    after(dve, "top2", p, 12)
                    dve.tensor_reduce(tv[:, 3], hit[:, 1], AX.X, ALU.max).then_inc(sems["top2"], 1)
                    after(dve, "top2", p, 13)
                    tt(ohot[:, 1], hit[:, 1], bc(tv[:, 3], EXPERTS), ALU.is_equal).then_inc(sems["top2"], 1)
                elif what == "top2_d":
                    after(dve, "top2_exp", p, 1)
                    ts(tv[:, 6], tv[:, 5], 1.0, None, ALU.add).then_inc(sems["top2"], 1)
                    after(dve, "top2", p, 15)
                    dve.reciprocal(tv[:, 7], tv[:, 6]).then_inc(sems["top2"], 1)
                    after(dve, "top2", p, 16)
                    tt(tv[:, 8], tv[:, 5], tv[:, 7], ALU.mult).then_inc(sems["gates"], 1)
                    tt(hit[:, 0], ohot[:, 0], bc(tv[:, 7], EXPERTS), ALU.mult).then_inc(sems["gates"], 1)
                    after(dve, "gates", p, 2)
                    tt(hit[:, 1], ohot[:, 1], bc(tv[:, 8], EXPERTS), ALU.mult).then_inc(sems["gates"], 1)
                    after(dve, "gates", p, 3)
                    tt(gate[:, par], hit[:, 0], hit[:, 1], ALU.add).then_inc(sems["gates"], 1)
                elif what == "gates_copy":
                    after(dve, "gates_turned", p, 1)
                    cp(gT[:].rearrange("p b t -> p (b t)"), F[:, 2, 0:2 * TOK]).then_inc(sems["gates_ready"], 1)
                elif what == "base":
                    for b in range(2):
                        after(dve, "bias2_ps", p, b + 1)
                        tt(base[:, par, b], x2[:, par, :, b, :], F[0:TOK, 2 + b, :].rearrange("p (c d) -> p c d", d=D),
                           ALU.add).then_inc(sems["base"], 1)

            def top(src, k, p, n0):
                dve.tensor_reduce(tv[:, k], src[:], AX.X, ALU.max).then_inc(sems["top2"], 1)
                after(dve, "top2", p, n0 + 1)
                tt(hit[:, k], src[:], bc(tv[:, k], EXPERTS), ALU.is_equal).then_inc(sems["top2"], 1)
                after(dve, "top2", p, n0 + 2)
                tt(hit[:, k], hit[:, k], rows(rev[:], 2 * NC), ALU.mult).then_inc(sems["top2"], 1)
                after(dve, "top2", p, n0 + 3)
                dve.tensor_reduce(tv[:, 2 + k], hit[:, k], AX.X, ALU.max).then_inc(sems["top2b"], 1)
                after(dve, "top2b", p, 1)
                tt(ohot[:, k], hit[:, k], bc(tv[:, 2 + k], EXPERTS), ALU.is_equal).then_inc(sems["top2"], 1)
                after(dve, "top2", p, n0 + 4)

            def ffn_step(p, par, n):
                if n % 2 == 1:
                    u = n // 2
                    g, ep = divmod(u, 8)
                    after(dve, "outputs_ps", p, n + 1)
                    gv = gate[:, par, 4 * g:4 * g + 4, 2 * ep:2 * ep + 2]
                    gv = gv.unsqueeze(3).to_broadcast([TOK, 4, 2, D])
                    src = O[0:TOK, u % 2, :].rearrange("p (c e d) -> p c e d", c=4, e=2)
                    if ep == 0:
                        after(dve, "folded", p, g - 1)
                        dst = acc[:, g % 2]
                    else:
                        after(dve, "added", p, max(7 * g + ep - TMPS, 0))
                        dst = tmp[:, (7 * g + ep) % TMPS].rearrange("p (c e d) -> p c e d", c=4, e=2)
                    tt(dst, src, gv, ALU.mult).then_inc(sems["gated"], 1)

            def final_step(what, b, p, par):
                if what == "f_sum":
                    after(dve, "summed", p, 2 * b + 2)
                    ln_sum(ys[:], fst, NC, "f_")
                elif what == "f_sub":
                    after(dve, "final", p, b)
                    ln_sub(ys[:], fxc[:], fst, NC, p, 3 * b, "f_")
                elif what == "f_var":
                    ln_var(fin[:, b], fst, NC, p, b, 3 * b, "f_")
                elif what == "f_gamma":
                    after(dve, "f_squared", p, b + 1)
                    tt(fxc[:], fxc[:], rows(gf_b[:], NC), ALU.mult).then_inc(sems["f_gamma"], 1)
                elif what == "f_apply":
                    after(dve, "f_gamma", p, b + 1)
                    after(dve, "f_rstd", p, b + 1)
                    tt(fxc[:], fxc[:], bc(fst[:, 4, 0:NC], D), ALU.mult).then_inc(sems["f_normed"], 1)
                elif what == "f_residual":
                    after(dve, "f_normed", p, b + 1)
                    after(dve, "f_beta", p, 1)
                    tt(fin[:, b], fxc[:], hres[:, par, :, b, :], ALU.add).then_inc(sems["final"], 1)

            run(dve, "dve", front_step, ffn_step, final_step, setup_step)

        @block.gpsimd
        def _(pool):
            tt = pool.tensor_tensor
            pool.memset(ones16[:], 1.0).then_inc(s_oned, 1)
            for w in (wemb, wg, wtok, wk, wq, wv, watt, b2d):
                m = pool.memset(w[:], 0.0)
            m.then_inc(s_wz, 1)
            pool.memset(ones[:], 1.0).then_inc(s_oned, 1)
            pool.memset(mhalf[:], -0.5).then_inc(s_half, 1)
            for e in range(EXPERTS):
                m = pool.memset(rev[:, e:e + 1], float(EXPERTS - e))
            m.then_inc(s_half, 1)
            pool.wait_ge(s_half, 2)
            pool.wait_ge(s_deg, 1)
            tt(dsrc[:], degc[:], mhalf[0:TB, 0:NB], ALU.pow).then_inc(s_dsrc, 1)
            pool.wait_ge(s_w, 16 * NW)

            def front_step(what, idx, p, par):
                if what == "ln_rstd":
                    after(pool, "variance", p, idx + 1)
                    tt(st[:, idx, 4], st[:, idx, 3], mhalf[0:TOK, 0:2 * NC], ALU.pow).then_inc(sems["rstd"], 1)
                elif what == "f_beta":
                    after(pool, "centred", p, 2)
                    tt(flat(hres[:, par]), flat(hres[:, par]), rows(bf_b[:], 2 * NC), ALU.add
                       ).then_inc(sems["f_beta"], 1)
                elif what == "hbeta":
                    if idx == 0:
                        after(pool, "tokens", p, 3)
                        after(pool, "hres", p, 0)
                        tt(flat(hb[:]), flat(hL[:]), rows(ba_b[:], 2 * NC), ALU.add).then_inc(sems["hbeta"], 1)

            def ffn_step(p, par, n):
                if n % 2 == 1:
                    u = n // 2
                    g, ep = divmod(u, 8)
                    if ep:
                        a = acc[:, g % 2].rearrange("p c e d -> p (c e d)")
                        after(pool, "gated", p, u + 1)
                        after(pool, "added", p, 7 * g + ep - 1)
                        tt(a, a, tmp[:, (7 * g + ep) % TMPS], ALU.add).then_inc(sems["added"], 1)
                    if ep == 7:
                        b, h = g // 2, g % 2
                        after(pool, "added", p, 7 * (g + 1))
                        if h == 0:
                            after(pool, "f_centred", p, b)
                        dst = ys[:, 4 * h:4 * h + 4, :]
                        tt(dst, acc[:, g % 2, :, 0, :], acc[:, g % 2, :, 1, :], ALU.add).then_inc(sems["folded"], 1)
                        after(pool, "folded", p, g + 1)
                        tt(dst, dst, base[:, par, b, 4 * h:4 * h + 4, :], ALU.add).then_inc(sems["summed"], 1)

            def final_step(what, b, p, par):
                if what == "f_rstd":
                    after(pool, "f_variance", p, b + 1)
                    tt(fst[:, 4, 0:NC], fst[:, 3, 0:NC], mhalf[0:TOK, 0:NC], ALU.pow).then_inc(sems["f_rstd"], 1)

            run(pool, "pool", front_step, ffn_step, final_step)


def constants():
    pos = np.arange(NODES, dtype=np.float32)[:, None]
    div = np.exp(np.arange(0, D, 2, dtype=np.float32) * np.float32(-math.log(10000.0) / D))
    pe = np.zeros((NODES, D), np.float32)
    pe[:, 0::2] = np.sin(pos * div)
    pe[:, 1::2] = np.cos(pos * div)
    head = np.arange(128) // DH
    return {
        "ident": np.eye(128, dtype=np.float32),
        "iota": np.broadcast_to(np.arange(NODES, dtype=np.float32), (128, NODES)).copy(),
        "mask": ((head[:, None] == head[None, :]) * SCALE).astype(np.float32),
        "pos": np.concatenate([pe.T, pe.T]),
    }


_INS = ["x", "txt", "L0_tok_W_embed", "L0_tok_b_embed", "L0_tok_W_gcn", "L0_tok_b_gcn", "L0_tok_W_out",
        "L0_tok_b_out", "L0_tok_edge_index", "L0_attn_Wqkv", "L0_attn_Wout", "L0_attn_bout", "L0_attn_gamma",
        "L0_attn_beta", "L0_ffn_gate_w", "L0_ffn_gate_b", "L0_ffn_w1", "L0_ffn_b1", "L0_ffn_w2", "L0_ffn_b2",
        "L0_ffn_gamma", "L0_ffn_beta"]


def kernel(**inputs):
    import concourse.bacc as _bacc
    from concourse.bass_utils import run_bass_kernel_spmd as _run

    nc = _bacc.Bacc("TRN2", target_bir_lowering=False, num_devices=1)
    arrays, args = {}, []
    for name in _INS:
        a = np.ascontiguousarray(inputs[name])
        arrays["in_" + name] = a
        args.append(nc.dram_tensor("in_" + name, a.shape, mybir.dt.from_np(a.dtype), kind="ExternalInput").ap())
    for name, a in constants().items():
        arrays["const_" + name] = a
        args.append(nc.dram_tensor("const_" + name, a.shape, mybir.dt.from_np(a.dtype), kind="ExternalInput").ap())
    out = nc.dram_tensor("out_0", (IMAGES, SEQ, D), F32, kind="ExternalOutput").ap()
    build(nc, *args, out)
    r = _run(nc, [arrays], core_ids=[0])
    return r.results[0]["out_0"]
```
